# Optimizing a Trainium2 kernel written in Bass

```python
import numpy as np
import jax
import jax.numpy as jnp

def _softmax(x, axis=-1):
    return jax.nn.softmax(x, axis=axis)

def _gelu(x):
    return jax.nn.gelu(x, approximate=True)

def _silu(x):
    return jax.nn.silu(x)

def _sigmoid(x):
    return jax.nn.sigmoid(x)

def _layernorm(x, axis=-1, eps=1e-05):
    m = jnp.mean(x, axis=axis, keepdims=True)
    v = jnp.var(x, axis=axis, keepdims=True)
    return (x - m) / jnp.sqrt(v + eps)

def _scatter_add(tgt, idx, src, axis=0):
    return tgt.at[idx].add(src)

def _segment_sum(src, seg, n):
    return jax.ops.segment_sum(src, seg, n)
kernel_name = 'mk_xattn_ffn_d1_seqx_r2_62bb82'

def setup_inputs(seed: int=0):
    np.random.seed(seed)
    _w = jnp.asarray

    def _rec_inputs():
        import jax
        import jax.numpy as jnp
        _rk = jax.random.key(seed)
        x = 7.22e-05 + 1 * jax.random.normal(jax.random.fold_in(_rk, 1), (2, 2048, 512), jnp.float32)
        _lenS = 2048 - jax.random.randint(jax.random.fold_in(_rk, 7), (2,), 0, max(1, 2048 // 4) + 1, jnp.int32)
        _lenS2 = 128 - jax.random.randint(jax.random.fold_in(_rk, 8), (2,), 0, max(1, 128 // 4) + 1, jnp.int32)
        _ctx_1024P = jax.random.normal(jax.random.fold_in(_rk, 11), (2, 16, 512), jnp.float32)
        _ctx_1024c = jax.random.dirichlet(jax.random.fold_in(_rk, 511), 0.3 * jnp.ones((16,), jnp.float32), (2, 128))
        _ctx_1024t = jnp.einsum('bsk,bkd->bsd', _ctx_1024c, _ctx_1024P)
        _ctx_1024t = _ctx_1024t * jax.lax.rsqrt(jnp.mean(jnp.square(_ctx_1024t)) + 1e-12) * 0.953939
        ctx_1024 = 4.13588e-05 + 0.999923 * (_ctx_1024t + 0.3 * jax.random.normal(jax.random.fold_in(_rk, 611), (2, 128, 512), jnp.float32))
        return (x, ctx_1024)
    x, ctx_1024 = _rec_inputs()

    def _L0_xattn_setup():
        import jax, jax.numpy as jnp
        import numpy as np
        EMBED_DIM = 512
        B, QL, KL = (4, 1024, 1024)
        key = jax.random.key(seed)
        k1, k2, k3, k4 = jax.random.split(key, 4)
        hidden_states = jax.random.normal(k1, (B, QL, EMBED_DIM), dtype=jnp.float32)
        decoder_hidden_states = jax.random.normal(k2, (B, KL, EMBED_DIM), dtype=jnp.float32)
        Wq = jax.random.normal(k3, (EMBED_DIM, EMBED_DIM), dtype=jnp.float32) * (1.0 / np.sqrt(EMBED_DIM))
        Wkv = jax.random.normal(k4, (EMBED_DIM, 2 * EMBED_DIM), dtype=jnp.float32) * (1.0 / np.sqrt(EMBED_DIM))
        return {'hidden_states': hidden_states, 'decoder_hidden_states': decoder_hidden_states, 'Wq': Wq, 'Wkv': Wkv}
    _L0_xattn_all = _L0_xattn_setup()
    _L0_xattn_in = {k: v for k, v in _L0_xattn_all.items() if k in ('Wq', 'Wkv')}
    del _L0_xattn_all

    def _L0_ffn_setup():
        import jax, jax.numpy as jnp
        import numpy as np
        BLOCK = 32
        W_BITS = 4
        ACT_BITS = 16

        def act_qdq(x):
            qmax = 2.0 ** (ACT_BITS - 1) - 1.0
            scale = jnp.maximum(jnp.max(jnp.abs(x)) / qmax, 1e-12)
            return jnp.clip(jnp.round(x / scale), -qmax - 1.0, qmax) * scale

        def fixed_qdq_u16(x):
            scale = 1.0 / 65536.0
            return jnp.clip(jnp.round(x / scale), 0.0, 65535.0) * scale

        def lpbq_dequant(w):
            O, I = w.shape
            qmax = 2.0 ** (W_BITS - 1) - 1.0
            wb = w.reshape(O, I // BLOCK, BLOCK)
            s = jnp.maximum(jnp.max(jnp.abs(wb), axis=-1, keepdims=True) / qmax, 1e-12)
            wq = jnp.clip(jnp.round(wb / s), -qmax - 1.0, qmax) * s
            return wq.reshape(O, I)
        key = jax.random.key(seed)
        k1, k2, k3, k4 = jax.random.split(key, 4)
        B, S, H, I = (2, 2048, 512, 1536)
        x = jax.random.normal(k1, (B, S, H), jnp.float32)
        w_gate = jax.random.normal(k2, (I, H), jnp.float32) * 0.02
        w_up = jax.random.normal(k3, (I, H), jnp.float32) * 0.02
        w_down = jax.random.normal(k4, (H, I), jnp.float32) * 0.02
        return {'x': x, 'w_gate': w_gate, 'w_up': w_up, 'w_down': w_down}
    _L0_ffn_all = _L0_ffn_setup()
    _L0_ffn_in = {k: v for k, v in _L0_ffn_all.items() if k in ('w_gate', 'w_up', 'w_down')}
    del _L0_ffn_all
    return {'x': x, 'ctx_1024': ctx_1024, 'L0_xattn_Wq': _L0_xattn_in['Wq'], 'L0_xattn_Wkv': _L0_xattn_in['Wkv'], 'L0_ffn_w_gate': _L0_ffn_in['w_gate'], 'L0_ffn_w_up': _L0_ffn_in['w_up'], 'L0_ffn_w_down': _L0_ffn_in['w_down']}

def reference(x, ctx_1024, L0_xattn_Wq, L0_xattn_Wkv, L0_ffn_w_gate, L0_ffn_w_up, L0_ffn_w_down):
    import jax
    import jax.numpy as jnp

    def _L0_xattn_ref(hidden_states, decoder_hidden_states, Wq, Wkv):
        import jax, jax.numpy as jnp
        import numpy as np
        EMBED_DIM = 512
        B, QL, KL = (4, 1024, 1024)
        d = Wq.shape[0]
        scale = 1.0 / np.sqrt(d)
        query = hidden_states @ Wq
        kv = decoder_hidden_states @ Wkv
        key, value = jnp.split(kv, 2, axis=-1)
        scores = jnp.einsum('bqd,bkd->bqk', query, key) * scale
        w = jax.nn.softmax(scores, axis=-1)
        return jnp.einsum('bqk,bkd->bqd', w, value)

    def _L0_ffn_ref(x, w_gate, w_up, w_down):
        import jax, jax.numpy as jnp
        import numpy as np
        BLOCK = 32
        W_BITS = 4
        ACT_BITS = 16

        def act_qdq(x):
            qmax = 2.0 ** (ACT_BITS - 1) - 1.0
            scale = jnp.maximum(jnp.max(jnp.abs(x)) / qmax, 1e-12)
            return jnp.clip(jnp.round(x / scale), -qmax - 1.0, qmax) * scale

        def fixed_qdq_u16(x):
            scale = 1.0 / 65536.0
            return jnp.clip(jnp.round(x / scale), 0.0, 65535.0) * scale

        def lpbq_dequant(w):
            O, I = w.shape
            qmax = 2.0 ** (W_BITS - 1) - 1.0
            wb = w.reshape(O, I // BLOCK, BLOCK)
            s = jnp.maximum(jnp.max(jnp.abs(wb), axis=-1, keepdims=True) / qmax, 1e-12)
            wq = jnp.clip(jnp.round(wb / s), -qmax - 1.0, qmax) * s
            return wq.reshape(O, I)
        x = act_qdq(x)
        up = act_qdq(x @ lpbq_dequant(w_up).T)
        gate = act_qdq(x @ lpbq_dequant(w_gate).T)
        sig = fixed_qdq_u16(jax.nn.sigmoid(gate))
        gate = act_qdq(gate * sig)
        o = act_qdq(gate * up)
        return o @ lpbq_dequant(w_down).T
    x = x + _L0_xattn_ref(_layernorm(x, axis=-1), ctx_1024, L0_xattn_Wq, L0_xattn_Wkv)
    x = x + _L0_ffn_ref(_layernorm(x, axis=-1), L0_ffn_w_gate, L0_ffn_w_up, L0_ffn_w_down)
    return x

_drawn_inputs = setup_inputs


def setup_inputs(seed=0):
    import zlib

    import numpy as np

    out = dict(_drawn_inputs(seed))
    spreads = {}
    factors = {}
    for name, (base, spread) in spreads.items():
        noise = np.random.default_rng([zlib.crc32(name.encode()), seed]).standard_normal(out[name].shape)
        drawn = base * np.exp(spread * noise) if base else spread * noise
        out[name] = jnp.asarray(drawn.astype(out[name].dtype))
    for name, factor in factors.items():
        out[name] = (out[name] * factor).astype(out[name].dtype)
    return out
```

```python
from contextlib import ExitStack

import concourse.bass as bass
from concourse import mybir

P = 128
B, S, D = 2, 2048, 512
KV = 128
I = 1536
T = B * S
EPS = 1e-5
QMAX = 32767.0
TINY = 1e-12
BLK = 32
NG = T // 512
TI = 4
KC = D // P
OC = I // P
UPG = OC // 2
NU = NG * UPG
GPB = NG // B
UW = 1024
NBLK = OC * D // BLK
SCALE = float(D) ** -0.5
ROUND = 12582912.0
WTOP = 2048.0

F32 = mybir.dt.float32
F16 = mybir.dt.float16
I16 = mybir.dt.int16
U16 = mybir.dt.uint16
I32 = mybir.dt.int32
ALU = mybir.AluOpType
ACT = mybir.ActivationFunctionType
AX = mybir.AxisListType
RMAX = bass.bass_isa.ReduceOp.max


def need(eng, sem, value):
    if isinstance(value, int) and value <= 0:
        return
    eng.wait_ge(sem, value)


def build(nc, x, ctx_in, wq_in, wkv_in, wg_in, wu_in, wd_in, out):
    x_v = x.rearrange("b (p j i) d -> b j p (i d)", p=P, j=GPB, i=TI)
    out_v = out.rearrange("b (p j i) d -> b j p (i d)", p=P, j=GPB, i=TI)
    gate_d = nc.dram_tensor("gate_park", [NU, P, UW], F32).ap()
    up_d = nc.dram_tensor("up_park", [NU, P, UW], F32).ap()
    x2_d = nc.dram_tensor("x2_park", [NG, P, TI * D], F32).ap()
    wd_d = nc.dram_tensor("wdown_park", [P, 12288], F16).ap()

    with ExitStack() as stack:
        def sem(name):
            return stack.enter_context(nc.semaphore(name))

        big = stack.enter_context(nc.sbuf_tensor("big", [P, 51200], F32))
        small = stack.enter_context(nc.sbuf_tensor("small", [P, 1800], F32))
        ps = stack.enter_context(nc.psum_tensor("ps", [P, 8, 512], F32))

        def part(start, words):
            return big[:, start:start + words]

        def cut(start, words):
            return small[:, start:start + words]

        X = part(0, 16384).rearrange("p (g i d) -> p g i d", g=NG, i=TI)
        XT = part(0, 16384).bitcast(F16).rearrange("p (g l k t) -> p g l k t", g=NG, l=2, k=KC)
        OT = part(0, 12288).bitcast(F16).rearrange("p (s l c t) -> p s l c t", s=2, l=2, c=OC)
        ring = part(12288, 4096).rearrange("p (s w) -> p s w", s=4)
        HT0 = 16384
        HT = part(HT0, 16384).rearrange("p (g k t) -> p g k t", g=NG, k=KC)
        cmean = part(HT0 + 2048, 128)
        ctx_sb = part(HT0 + 4096, 1024).rearrange("p (b d) -> p b d", b=B)
        ctxT = part(HT0 + 5120, 1024).rearrange("p (k b s) -> p k b s", k=KC, b=B)
        KT = part(HT0 + 6144, 1024).rearrange("p (k s) -> p k s", k=KC)
        Mraw = part(HT0 + 7168, 1024).rearrange("p (k s) -> p k s", k=KC)
        wkv = part(HT0 + 8192, 4096).rearrange("p (k n) -> p k n", k=KC)
        wqT = part(HT0 + 12288, 2048).rearrange("p (k n) -> p k n", k=KC)
        wq = part(HT0 + 14336, 2048).rearrange("p (k n) -> p k n", k=KC)
        gate_out = part(HT0, 2048).rearrange("p (s w) -> p s w", s=2)
        wd_prep = part(HT0 + 2048, 6144).bitcast(F16).rearrange("p (l c n) -> p l c n", l=2, c=OC)
        WG = part(32768, 6144).bitcast(F16).rearrange("p (l k o) -> p l k o", l=2, k=KC)
        WN = part(38912, 6144)
        U0 = 45056
        WU = part(U0, 6144).bitcast(F16).rearrange("p (l k o) -> p l k o", l=2, k=KC)
        WD = part(U0, 6144).bitcast(F16).rearrange("p (l c n) -> p l c n", l=2, c=OC)
        M = part(U0, 1024).rearrange("p (k b s) -> p k b s", k=KC, b=B)
        V = part(U0 + 1024, 1024).rearrange("p (b d) -> p b d", b=B)
        xTs = part(U0 + 2048, 1024).rearrange("p (s k t) -> p s k t", s=2, k=KC)
        Pe = part(U0 + 3072, 512).rearrange("p (i s) -> p i s", i=TI)
        PTs = part(U0 + 3584, 512).rearrange("p (i t) -> p i t", i=TI)
        h2 = part(U0 + 4096, 2048).rearrange("p (s d) -> p s d", s=4)
        hq = part(U0, 2048).bitcast(I16).rearrange("p (s w) -> p s w", s=2)
        Q = part(HT0, 24576).bitcast(I16).rearrange("p (u w) -> p u w", u=NU)
        up_out = part(40960, 2048).rearrange("p (s w) -> p s w", s=2)
        gate_in = part(43008, 2048).rearrange("p (s w) -> p s w", s=2)
        qa = part(40960, 1024).bitcast(I16).rearrange("p (s w) -> p s w", s=2)
        qb = part(41984, 1024).bitcast(I16).rearrange("p (s w) -> p s w", s=2)
        x2_in = part(43008, 2048).rearrange("p (s w) -> p s w", s=2)

        bn = cut(0, 192).rearrange("p (n s) -> p n s", n=32)
        mv = cut(192, 64).rearrange("p (n s) -> p n s", n=32)
        ve = cut(256, 32)
        rs1 = cut(288, 32)
        nmax = cut(320, 32)
        rsum = cut(352, 32)
        rinv = cut(384, 32)
        negm = cut(416, 32)
        rs2 = cut(448, 32)
        smax = cut(480, 32)
        half = cut(512, 32)
        bmax = cut(544, 192)
        binv = cut(736, 192)
        bscl = cut(928, 192)
        ident = cut(1120, 128)
        aq = cut(0, 1024).bitcast(I16).rearrange("p (s w) -> p s w", s=2)
        sigq = cut(1024, 512).bitcast(U16)
        hcol = cut(1536, 8)
        gcol = cut(1544, 48)
        ucol = cut(1592, 48)
        scol = cut(1640, 2)
        ocol = cut(1688, 12)
        sc = cut(1736, 64)

        names = ("hmx hall gmx gall umx uall smx sall omx oall wmx0 wall0 wmx1 wall1 wmx2 wall2 "
                 "pw0 pw1 pw2 rpw xs xinv fg gt gsc grc ginv fu usc uinv ut urc st ssc sinv src su ot osc "
                 "oinv orc oo fin0 fin").split()
        col = {n: sc[:, k:k + 1] for k, n in enumerate(names)}

        x_ld = [sem(f"x_ld{g}") for g in range(NG)]
        ctx_ld, wq_ld, wkv_ld = sem("ctx_ld"), sem("wq_ld"), sem("wkv_ld")
        wn_ld = [sem(f"wn_ld{m}") for m in range(3)]
        consts = sem("consts")
        pro_mm, pro_ev, pro_c = sem("pro_mm"), sem("pro_ev"), sem("pro_c")
        stat1, ve1_d, rs1_d = sem("stat1"), sem("ve1_d"), sem("rs1_d")
        xt_mm, xt_ev, sc_mm, nmax_d, exp_d = sem("xt_mm"), sem("xt_ev"), sem("sc_mm"), sem("nmax_d"), sem("exp_d")
        smax_d, rinv_d = sem("smax_d"), sem("rinv_d")
        pt_mm, pt_ev, av_mm, x2_d_s = sem("pt_mm"), sem("pt_ev"), sem("av_mm"), sem("x2_done")
        bn2_d, mv2_d, ve2_d, rs2_d, h2_d = sem("bn2_d"), sem("mv2_d"), sem("ve2_d"), sem("rs2_d"), sem("h2_d")
        ht_mm, ht_ev, hcol_d, x2_st = sem("ht_mm"), sem("ht_ev"), sem("hcol_d"), sem("x2_st")
        w_blk, w_inv, w_rnd, w_deq = sem("w_blk"), sem("w_inv"), sem("w_rnd"), sem("w_deq")
        wt_mm, wt_hi, wt_lo, wd_st, wd_ld = sem("wt_mm"), sem("wt_hi"), sem("wt_lo"), sem("wd_st"), sem("wd_ld")
        link = sem("link")
        col_max, col_all = sem("col_max"), sem("col_all")
        xinv_d, hq_d, hhi_d, hlo_d = sem("xinv_d"), sem("hq_d"), sem("hhi_d"), sem("hlo_d")
        g_mm, g_ev, g_mx = sem("g_mm"), sem("g_ev"), sem("g_mx")
        g_st = [sem("g_st0"), sem("g_st1")]
        u_mm, u_ev, u_mx = sem("u_mm"), sem("u_ev"), sem("u_mx")
        u_st = [sem("u_st0"), sem("u_st1")]
        g_ld = [sem("g_ld0"), sem("g_ld1")]
        ginv_d, q_d, aq_d, sig_d, r_d, a_mx, b_d = (sem(n) for n in
                                                  ("ginv_d", "q_d", "aq_d", "sig_d", "r_d", "a_mx", "b_d"))
        uinv_d, au_d, ag_d, agv_d, o_mx = (sem(n) for n in ("uinv_d", "au_d", "ag_d", "agv_d", "o_mx"))
        r5_ld = [sem(f"r5_ld{s}") for s in range(4)]
        r6_ld = [sem(f"r6_ld{s}") for s in range(4)]
        uq_d, oq_d, ohi_d, olo_d = sem("uq_d"), sem("oq_d"), sem("ohi_d"), sem("olo_d")
        dn_mm, fin_d = sem("dn_mm"), sem("fin_d")
        x2_ld = [sem("x2_ld0"), sem("x2_ld1")]
        out_st = [sem("out_st0"), sem("out_st1")]

        block = stack.enter_context(nc.Block())

        def batch(g):
            return g // GPB

        @block.sync
        def _(sp):
            sp.dma_start(ctx_sb, ctx_in.rearrange("b s d -> s b d")).then_inc(ctx_ld, 16)
            sp.dma_start(wkv, wkv_in.rearrange("(k p) n -> p k n", p=P)).then_inc(wkv_ld, 16)
            for g in range(NG):
                sp.dma_start(X[:, g].rearrange("p i d -> p (i d)"), x_v[g // GPB, g % GPB]).then_inc(x_ld[g], 16)
                if g == 0:
                    sp.dma_start(wq, wq_in.rearrange("(k p) n -> p k n", p=P)).then_inc(wq_ld, 16)
                if g == 1:
                    sp.dma_start(WN.rearrange("p (c d) -> p c d", c=OC),
                                 wg_in.rearrange("(c p) d -> p c d", p=P)).then_inc(wn_ld[0], 16)
            with nc.sync.Fori(0, NG) as g:
                sp.wait_ge(x2_d_s, TI * g + TI)
                sp.dma_start(x2_d[g], X[:, g].rearrange("p i d -> p (i d)")).then_inc(x2_st, 16)
            sp.wait_ge(wt_lo, OC)
            sp.dma_start(WN.rearrange("p (c d) -> p c d", c=OC),
                         wu_in.rearrange("(c p) d -> p c d", p=P)).then_inc(wn_ld[1], 16)

            def park_gate(g):
                for n in range(UPG):
                    sp.wait_ge(g_ev, g * UPG + n + 1)
                    sp.dma_start(gate_d[g * UPG + n], gate_out[:, n % 2]).then_inc(g_st[n % 2], 16)

            with nc.sync.Fori(0, 4) as g:
                park_gate(g)
            sp.wait_ge(wt_lo, 2 * OC)
            sp.dma_start(WN.rearrange("p (h n) -> p h n", h=KC),
                         wd_in.rearrange("(h p) n -> p h n", p=P)).then_inc(wn_ld[2], 16)
            with nc.sync.Fori(4, NG) as g:
                park_gate(g)
            sp.wait_ge(wt_lo, 3 * OC)
            sp.dma_start(wd_d, wd_prep.rearrange("p l c n -> p (l c n)")).then_inc(wd_st, 16)
            for s in range(2):
                sp.wait_ge(g_st[s], 16 * NU // 2)

            def fetch_gate(v, s, first):
                if not first:
                    sp.wait_ge(a_mx, v - 1)
                sp.dma_start(gate_in[:, s], gate_d[v]).then_inc(g_ld[s], 16)

            def park_up(n, s):
                sp.wait_ge(u_ev, n + 1)
                sp.dma_start(up_d[n], up_out[:, s]).then_inc(u_st[s], 16)

            sp.wait_ge(wt_lo, 3 * OC)
            for s in range(2):
                fetch_gate(s, s, True)
            with nc.sync.Fori(0, 11) as t:
                for s in range(2):
                    park_up(2 * t + s, s)
                    for r in range(2):
                        fetch_gate(4 * t + 2 * s + r + 2, r, False)
            park_up(22, 0)
            for r in range(2):
                fetch_gate(46 + r, r, False)
            park_up(23, 1)
            with nc.sync.Fori(12, 24) as t:
                for s in range(2):
                    park_up(2 * t + s, s)
            sp.wait_ge(wd_st, 16)
            sp.wait_ge(u_mm, NU)
            sp.dma_start(WD.rearrange("p l c n -> p (l c n)"), wd_d).then_inc(wd_ld, 16)
            for s in range(2):
                sp.wait_ge(u_st[s], 16 * NU // 2)
            for s in range(4):
                sp.dma_start(ring[:, s], up_d[s]).then_inc(r5_ld[s], 16)
            with nc.sync.Fori(1, NU // 4) as t:
                for s in range(4):
                    sp.wait_ge(o_mx, 4 * t + s - 3)
                    sp.dma_start(ring[:, s], up_d[4 * t + s]).then_inc(r5_ld[s], 16)
            for s in range(4):
                sp.wait_ge(o_mx, NU - 3 + s)
                sp.dma_start(ring[:, s], up_d[s]).then_inc(r6_ld[s], 16)
            sp.wait_ge(x2_st, 16 * NG)
            sp.wait_ge(b_d, NU)

            def fetch_x2(g, r):
                sp.dma_start(x2_in[:, r], x2_d[g, :, r * UW:(r + 1) * UW]).then_inc(x2_ld[r], 16)

            def store_out(b, j, g, r):
                sp.wait_ge(fin_d, 2 * g + r + 1)
                sp.dma_start(out_v[b, j, :, r * UW:(r + 1) * UW], x2_in[:, r]).then_inc(out_st[r], 16)

            def fetch_up(n, s):
                sp.wait_ge(uq_d, n - 3)
                sp.dma_start(ring[:, s], up_d[n]).then_inc(r6_ld[s], 16)

            for r in range(2):
                fetch_x2(0, r)
            for n in range(4, 2 * UPG):
                fetch_up(n, n % 4)
            for s in range(2):
                for n in range(UPG):
                    fetch_up((s + 2) * UPG + n, (s * UPG + n) % 4)
                for r in range(2):
                    store_out(0, s, s, r)
                for r in range(2):
                    sp.wait_ge(out_st[r], 16 * (s + 1))
                    fetch_x2(s + 1, r)
            with nc.sync.Fori(1, 3) as t:
                for s in range(2):
                    g = 2 * t + s
                    for n in range(UPG):
                        fetch_up((g + 2) * UPG + n, (s * UPG + n) % 4)
                    for r in range(2):
                        store_out(batch(g), g % GPB, g, r)
                    for r in range(2):
                        sp.wait_ge(out_st[r], 16 * (g + 1))
                        fetch_x2(g + 1, r)
            for g in range(NG - 2, NG):
                for r in range(2):
                    store_out(g // GPB, g % GPB, g, r)
                if g < NG - 1:
                    for r in range(2):
                        sp.wait_ge(out_st[r], 16 * (g + 1))
                        fetch_x2(g + 1, r)
            for r in range(2):
                sp.wait_ge(out_st[r], 16 * NG)

        @block.gpsimd
        def _(pool):
            nc.gpsimd.memset(ident, 0.0).then_inc(consts, 1)
            nc.gpsimd.memset(half, -0.5).then_inc(consts, 1)
            nc.gpsimd.memset(cmean, 1.0 / D).then_inc(consts, 1)
            pool.wait_ge(consts, 1)
            nc.gpsimd.affine_select(out=ident, in_=ident, compare_op=ALU.not_equal, fill=1.0, base=0,
                                    pattern=[[-1, P]], channel_multiplier=1).then_inc(consts, 1)
            pool.wait_ge(consts, 4)
            for g in range(NG):
                r = rs1[:, TI * g:TI * g + TI]
                pool.wait_ge(ve1_d, g + 1)
                nc.gpsimd.tensor_tensor(r, ve[:, TI * g:TI * g + TI], half[:, TI * g:TI * g + TI],
                                        ALU.pow).then_inc(rs1_d, 1)
                pool.wait_ge(rs1_d, 2 * g + 1)
                nc.gpsimd.tensor_scalar(r, r, SCALE, 1.0, ALU.mult, ALU.mult).then_inc(rs1_d, 1)

            def all_max(k, src, dst):
                pool.wait_ge(col_max, k + 1)
                nc.gpsimd.partition_all_reduce(col[dst], col[src], P, RMAX).then_inc(col_all, 1)

            def quant_weights(at, blocks, base):
                w = WN[:, bass.ds(at * blocks * BLK, blocks * BLK)]
                wb = w.rearrange("p (n e) -> p n e", e=BLK)
                inv = binv[:, bass.ds(at * blocks, blocks)].unsqueeze(2).to_broadcast([P, blocks, BLK])
                scl = bscl[:, bass.ds(at * blocks, blocks)].unsqueeze(2).to_broadcast([P, blocks, BLK])
                nc.gpsimd.tensor_tensor(wb, wb, inv, ALU.mult).then_inc(w_inv, 1)
                pool.wait_ge(w_inv, base + at + 1)
                nc.gpsimd.tensor_scalar(w, w, ROUND, 1.0, ALU.add, ALU.mult).then_inc(w_rnd, 1)
                pool.wait_ge(w_rnd, 2 * base + 2 * at + 1)
                nc.gpsimd.tensor_scalar(w, w, -ROUND, 1.0, ALU.add, ALU.mult).then_inc(w_rnd, 1)
                pool.wait_ge(w_rnd, 2 * base + 2 * at + 2)
                nc.gpsimd.tensor_tensor(wb, wb, scl, ALU.mult).then_inc(w_deq, 1)

            def normalise(g):
                c = bass.ds(TI * g, TI)
                pool.wait_ge(ve2_d, g + 1)
                nc.gpsimd.tensor_tensor(rs2[:, c], ve[:, c], half[:, c], ALU.pow).then_inc(rs2_d, 1)
                pool.wait_ge(rs2_d, g + 1)
                for i in range(TI):
                    need(pool, ht_mm, TI * g + i - 3)
                    nc.gpsimd.tensor_scalar(h2[:, i], X[:, g, i], negm[:, bass.ds(TI * g + i, 1)],
                                            rs2[:, bass.ds(TI * g + i, 1)], ALU.add, ALU.mult).then_inc(h2_d, 1)

            all_max(0, "wmx0", "wall0")
            pool.wait_ge(w_blk, 1)
            quant_weights(0, NBLK // 8, 0)
            normalise(0)
            for g in range(1, NG):
                quant_weights(g, NBLK // 8, 0)
                normalise(g)
            all_max(1, "hmx", "hall")
            all_max(2, "wmx1", "wall1")
            pool.wait_ge(w_blk, 2)
            quant_weights(0, NBLK, 8)
            all_max(3, "wmx2", "wall2")
            pool.wait_ge(w_blk, 3)
            quant_weights(0, NBLK, 9)
            all_max(4, "gmx", "gall")
            pool.wait_ge(ginv_d, 1)
            pool.wait_ge(wd_st, 16)
            for v in range(NU):
                pool.wait_ge(g_ld[v % 2], 16 * (v // 2) + 16)
                nc.gpsimd.tensor_scalar(Q[:, v], gate_in[:, v % 2], col["ginv"], 1.0,
                                        ALU.mult, ALU.mult).then_inc(q_d, 1)
            all_max(5, "smx", "sall")
            all_max(6, "umx", "uall")
            all_max(7, "omx", "oall")

        @block.tensor
        def _(pe):
            def turn(dst, src):
                return nc.tensor.transpose(dst, src, ident)

            pe.wait_ge(consts, 4)
            pe.wait_ge(ctx_ld, 16)
            for b in range(B):
                for k in range(KC):
                    mm = turn(ps[:, b, k * P:(k + 1) * P], ctx_sb[:, b, k * P:(k + 1) * P])
                mm.then_inc(pro_mm, 1)
            pe.wait_ge(wkv_ld, 16)
            pe.wait_ge(pro_ev, 2)
            for m in range(KC):
                for k in range(KC):
                    mm = nc.tensor.matmul(ps[:, 2 + m // 2, (m % 2) * 256:(m % 2) * 256 + 256],
                                          wkv[:, k, m * P:(m + 1) * P],
                                          ctxT[:, k].rearrange("p b s -> p (b s)"), start=(k == 0), stop=(k == KC - 1))
                if m % 2:
                    mm.then_inc(pro_mm, 1)
            pe.wait_ge(wq_ld, 16)
            for k in range(KC):
                for m in range(KC):
                    mm = turn(ps[:, 4 + k, m * P:(m + 1) * P], wq[:, k, m * P:(m + 1) * P])
                mm.then_inc(pro_mm, 1)
            for b in range(B):
                for k in range(KC):
                    mm = nc.tensor.matmul(ps[:, b], ctxT[:, k, b], wkv[:, k, D:2 * D],
                                          start=(k == 0), stop=(k == KC - 1))
                mm.then_inc(pro_mm, 1)
            pe.wait_ge(pro_ev, 8)
            for h in range(KC):
                for m in range(KC):
                    mm = nc.tensor.matmul(ps[:, 2 + h // 2, (h % 2) * 256:(h % 2) * 256 + 256],
                                          wqT[:, m, h * P:(h + 1) * P], KT[:, m],
                                          start=(m == 0), stop=(m == KC - 1))
                if h % 2:
                    mm.then_inc(pro_mm, 1)
            pe.wait_ge(pro_ev, 12)
            for k in range(KC):
                mm = nc.tensor.matmul(ps[:, 4, 0:256], cmean, Mraw[:, k], start=(k == 0), stop=(k == KC - 1))
            mm.then_inc(pro_mm, 1)
            pe.wait_ge(pro_c, 1)

            def scores(g):
                def turn_x(i):
                    need(pe, xt_ev, TI * g + i - 1)
                    for k in range(KC):
                        mm = turn(ps[:, i % 2, k * P:(k + 1) * P], X[:, g, i, k * P:(k + 1) * P])
                    mm.then_inc(xt_mm, 1)

                turn_x(0)
                for i in range(TI):
                    if i + 1 < TI:
                        turn_x(i + 1)
                    if i == 0:
                        need(pe, exp_d, TI * g)
                    pe.wait_ge(xt_ev, TI * g + i + 1)
                    for k in range(KC):
                        mm = nc.tensor.matmul(ps[:, 2, i * P:(i + 1) * P], xTs[:, i % 2, k], M[:, k, batch(g)],
                                              start=(k == 0), stop=(k == KC - 1))
                mm.then_inc(sc_mm, 1)

            def attend(g):
                need(pe, pt_ev, g)
                for i in range(TI):
                    pe.wait_ge(exp_d, TI * g + i + 1)
                    mm = turn(ps[:, 3, i * P:(i + 1) * P], Pe[:, i])
                mm.then_inc(pt_mm, 1)
                pe.wait_ge(pt_ev, g + 1)
                for i in range(TI):
                    need(pe, x2_d_s, TI * g + i - 1)
                    nc.tensor.matmul(ps[:, 4 + i % 2], PTs[:, i], V[:, batch(g)],
                                     start=True, stop=True).then_inc(av_mm, 1)

            def turn_h(g):
                for i in range(TI):
                    need(pe, ht_ev, TI * g + i - 1)
                    pe.wait_ge(h2_d, TI * g + i + 1)
                    for k in range(KC):
                        mm = turn(ps[:, 6 + i % 2, k * P:(k + 1) * P], h2[:, i, k * P:(k + 1) * P])
                    mm.then_inc(ht_mm, 1)

            def turn_weights(m, c, bank, gap):
                if c == 0:
                    pe.wait_ge(w_deq, 8 + m)
                if c >= gap:
                    pe.wait_ge(wt_lo, m * OC + c - gap + 1)
                for k in range(KC):
                    at = k * I + c * P if m == 2 else c * D + k * P
                    mm = turn(ps[:, bank, k * P:(k + 1) * P], WN[:, at:at + P])
                mm.then_inc(wt_mm, 1)

            scores(0)
            scores(1)
            attend(0)
            scores(2)
            attend(1)
            turn_h(0)
            for g in range(3, NG):
                scores(g)
                attend(g - 1)
                turn_h(g - 2)
            attend(NG - 1)
            turn_h(NG - 2)
            pe.wait_ge(exp_d, TI * NG)
            for c in range(OC):
                turn_weights(0, c, c % 3, 3)
            turn_h(NG - 1)

            def unit(w, g, n, done):
                for j in range(2):
                    o = (2 * n + j) * P
                    for k in range(KC):
                        for a, b in ((0, 0), (1, 0), (0, 1)):
                            mm = nc.tensor.matmul(ps[:, 2 * (n % 2) + j], w[:, a, k, o:o + P], XT[:, g, b, k],
                                                  start=(k == 0 and a + b == 0), stop=(k == KC - 1 and b == 1))
                mm.then_inc(done, 1)

            def product(w, g, mm_sem, ev_sem, turned=None):
                for n in range(UPG):
                    need(pe, ev_sem, g * UPG + n - 1)
                    unit(w, g, n, mm_sem)
                    if turned is not None:
                        for c in (2 * n, 2 * n + 1):
                            turn_weights(turned, c, 4 + c % 4, 4)

            def gate(g, turned=None):
                pe.wait_ge(hlo_d, g + 1)
                product(WG, g, g_mm, g_ev, turned)

            pe.wait_ge(wt_lo, OC)
            gate(0)
            with nc.tensor.Fori(1, 3) as g:
                gate(g)
            gate(3, 1)
            with nc.tensor.Fori(4, 7) as g:
                gate(g)
            gate(7, 2)
            pe.wait_ge(wt_lo, 2 * OC)
            pe.wait_ge(g_ev, NU)
            product(WU, 0, u_mm, u_ev)
            with nc.tensor.Fori(1, NG) as g:
                product(WU, g, u_mm, u_ev)

            def down(g, s):
                need(pe, fin_d, 2 * g - 2)
                for n in range(UPG):
                    pe.wait_ge(olo_d, g * UPG + n + 1)
                    for i in range(TI):
                        for c in (2 * n, 2 * n + 1):
                            for a, b in ((0, 0), (0, 1), (1, 0)):
                                mm = nc.tensor.matmul(ps[:, 4 * s + i], OT[:, s, a, c, i * P:(i + 1) * P], WD[:, b, c],
                                                      start=(c == 0 and a + b == 0), stop=(c == OC - 1 and a == 1))
                        if n == UPG - 1 and i % 2:
                            mm.then_inc(dn_mm, 1)

            pe.wait_ge(wd_ld, 16)
            pe.wait_ge(u_ev, NU)
            down(0, 0)
            down(1, 1)
            with nc.tensor.Fori(1, NG // 2) as t:
                for s in range(2):
                    down(2 * t + s, s)

        @block.scalar
        def _(act):
            def copy(dst, src):
                return nc.scalar.activation(dst, src, ACT.Copy)

            for b in range(B):
                act.wait_ge(pro_mm, b + 1)
                copy(ctxT[:, :, b], ps[:, b].rearrange("p (k s) -> p k s", k=KC)).then_inc(pro_ev, 1)
            for m in range(2):
                act.wait_ge(pro_mm, m + 3)
                copy(KT[:, 2 * m:2 * m + 2], ps[:, 2 + m].rearrange("p (k s) -> p k s", k=2)).then_inc(pro_ev, 1)
            for k in range(KC):
                act.wait_ge(pro_mm, k + 5)
                copy(wqT[:, :, k * P:(k + 1) * P], ps[:, 4 + k].rearrange("p (m s) -> p m s", m=KC)).then_inc(pro_ev, 1)
            for b in range(B):
                act.wait_ge(pro_mm, b + 9)
                copy(V[:, b], ps[:, b]).then_inc(pro_ev, 1)
            for m in range(2):
                act.wait_ge(pro_mm, m + 11)
                copy(Mraw[:, 2 * m:2 * m + 2], ps[:, 2 + m].rearrange("p (k s) -> p k s", k=2)).then_inc(pro_ev, 1)

            def take_xT(g):
                for i in range(TI):
                    act.wait_ge(xt_mm, TI * g + i + 1)
                    copy(xTs[:, i % 2], ps[:, i % 2].rearrange("p (k t) -> p k t", k=KC)).then_inc(xt_ev, 1)

            def take_pT(g):
                act.wait_ge(pt_mm, g + 1)
                need(act, av_mm, TI * g)
                copy(PTs, ps[:, 3].rearrange("p (i t) -> p i t", i=TI)).then_inc(pt_ev, 1)

            def take_hT(g):
                for i in range(TI):
                    act.wait_ge(ht_mm, TI * g + i + 1)
                    copy(HT[:, g, :, i * P:(i + 1) * P], ps[:, 6 + i % 2].rearrange("p (k t) -> p k t", k=KC)).then_inc(ht_ev, 1)

            def exps(g):
                act.wait_ge(nmax_d, g + 1)
                need(act, pt_mm, g)
                for i in range(TI):
                    n = bass.ds(TI * g + i, 1)
                    nc.scalar.activation(Pe[:, i], ps[:, 2, i * P:(i + 1) * P], ACT.Exp, bias=nmax[:, n],
                                         scale=rs1[:, n], accum_out=rsum[:, n]).then_inc(exp_d, 1)

            take_xT(0)
            exps(0)
            take_xT(1)
            take_pT(0)
            exps(1)
            with nc.scalar.Fori(2, NG) as g:
                take_xT(g)
                take_pT(g - 1)
                take_hT(g - 2)
                exps(g)
            take_pT(NG - 1)
            take_hT(NG - 2)

            def weights_hi(m, c, bank):
                act.wait_ge(wt_mm, m * OC + c + 1)
                src = ps[:, bank]
                if m == 2:
                    dst = wd_prep[:, 0, c]
                else:
                    dst = (WG, WU)[m][:, 0, :, c * P:(c + 1) * P]
                    src = src.rearrange("p (k o) -> p k o", k=KC)
                copy(dst, src).then_inc(wt_hi, 1)

            for c in range(OC):
                weights_hi(0, c, c % 3)
            take_hT(NG - 1)

            act.wait_ge(xinv_d, 1)
            for g in range(NG):
                if g >= 2:
                    act.wait_ge(hlo_d, g - 1)
                nc.scalar.activation(hq[:, g % 2], HT[:, g].rearrange("p k t -> p (k t)"), ACT.Copy,
                                     scale=col["xinv"]).then_inc(hq_d, 1)

            def take_gate(g, turned=None):
                for n in range(UPG):
                    act.wait_ge(g_mm, g * UPG + n + 1)
                    need(act, g_mx, g * UPG + n - 1)
                    if not (isinstance(g, int) and g == 0 and n < 2):
                        act.wait_ge(g_st[n % 2], 16 * (g * (UPG // 2) + n // 2))
                    copy(gate_out[:, n % 2], ps[:, 2 * (n % 2):2 * (n % 2) + 2].rearrange("p b w -> p (b w)")).then_inc(g_ev, 1)
                    if turned is not None:
                        for c in (2 * n, 2 * n + 1):
                            weights_hi(turned, c, 4 + c % 4)

            take_gate(0)
            with nc.scalar.Fori(1, 3) as g:
                take_gate(g)
            take_gate(3, 1)
            with nc.scalar.Fori(4, 7) as g:
                take_gate(g)
            take_gate(7, 2)

            def take_up(n, s, first):
                act.wait_ge(u_mm, n + 1)
                if not first:
                    act.wait_ge(u_mx, n - 1)
                    act.wait_ge(u_st[s], 8 * (n - s))
                copy(up_out[:, s], ps[:, 2 * s:2 * s + 2].rearrange("p b w -> p (b w)")).then_inc(u_ev, 1)

            def sweep_a(v, s, first):
                act.wait_ge(g_ld[s], 8 * (v - s) + 16)
                if not first:
                    act.wait_ge(a_mx, v - 1)
                nc.scalar.activation(aq[:, s], gate_in[:, s], ACT.Abs, scale=col["ginv"]).then_inc(aq_d, 1)
                act.wait_ge(q_d, v + 1)
                act.wait_ge(aq_d, v + 1)
                nc.scalar.activation(gate_in[:, s], Q[:, v], ACT.Sigmoid, scale=col["gsc"]).then_inc(sig_d, 1)

            def sweep_b(v, s, first):
                if first:
                    act.wait_ge(a_mx, NU - 1 + s)
                else:
                    act.wait_ge(r_d, NU + v - 1)
                nc.scalar.activation(gate_in[:, s], Q[:, v], ACT.Sigmoid, scale=col["gsc"]).then_inc(sig_d, 1)

            act.wait_ge(ginv_d, 1)
            act.wait_ge(wt_lo, 3 * OC)
            sweep_a(0, 0, True)
            take_up(0, 0, True)
            sweep_a(1, 1, True)
            sweep_a(2, 0, False)
            take_up(1, 1, True)
            sweep_a(3, 1, False)
            with nc.scalar.Fori(1, 12) as t:
                for s in range(2):
                    sweep_a(4 * t + 2 * s, 0, False)
                    take_up(2 * t + s, s, False)
                    sweep_a(4 * t + 2 * s + 1, 1, False)
            sweep_b(0, 0, True)
            take_up(24, 0, False)
            sweep_b(1, 1, True)
            sweep_b(2, 0, False)
            take_up(25, 1, False)
            sweep_b(3, 1, False)
            with nc.scalar.Fori(13, 24) as t:
                for s in range(2):
                    sweep_b(4 * t - 48 + 2 * s, 0, False)
                    take_up(2 * t + s, s, False)
                    sweep_b(4 * t - 48 + 2 * s + 1, 1, False)

            act.wait_ge(uinv_d, 1)
            act.wait_ge(b_d, NU)

            def magnitudes(t, k):
                s = k % 4
                n = 12 * t + k
                act.wait_ge(r5_ld[s], 16 * (3 * t + k // 4) + 16)
                need(act, o_mx, n - 1)
                nc.scalar.activation(qa[:, k % 2], ring[:, s], ACT.Abs, scale=col["uinv"]).then_inc(au_d, 1)
                if k % 3 != 2:
                    nc.scalar.activation(qb[:, k % 2], Q[:, n], ACT.Abs).then_inc(ag_d, 1)

            for k in range(12):
                magnitudes(0, k)
            with nc.scalar.Fori(1, 4) as t:
                for k in range(12):
                    magnitudes(t, k)

            def up_int(t, k):
                s = k % 4
                n = 12 * t + k
                act.wait_ge(r6_ld[s], 16 * (3 * t + k // 4) + 16)
                need(act, oq_d, n - 1)
                nc.scalar.activation(qa[:, k % 2], ring[:, s], ACT.Copy, scale=col["uinv"]).then_inc(uq_d, 1)

            act.wait_ge(o_mx, NU)
            for k in range(12):
                up_int(0, k)
            with nc.scalar.Fori(1, 4) as t:
                for k in range(12):
                    up_int(t, k)

        @block.vector
        def _(dve):
            count = [0]

            def linked(ins):
                count[0] += 1
                ins.then_inc(link, 1)
                dve.wait_ge(link, count[0])

            def scalar2(dst, src, s1, s2, op0=ALU.mult, op1=ALU.mult):
                linked(nc.vector.tensor_scalar(dst, src, s1, s2, op0, op1))

            linked(nc.vector.memset(scol, 0.0))
            linked(nc.vector.memset(ocol, 0.0))
            for g in range(NG):
                dve.wait_ge(x_ld[g], 16)
                for i in range(TI):
                    last = nc.vector.bn_stats(bn[:, TI * g + i], X[:, g, i])
                linked(last)
                for i in range(TI):
                    last = nc.vector.bn_aggr(mv[:, TI * g + i], bn[:, TI * g + i])
                linked(last)
                nc.vector.tensor_scalar(ve[:, TI * g:TI * g + TI], mv[:, TI * g:TI * g + TI, 1], EPS, None,
                                        ALU.add).then_inc(ve1_d, 1)
                if g == 3:
                    dve.wait_ge(pro_mm, 13)
                    dve.wait_ge(pro_ev, 12)
                    mean = ps[:, 4, 0:256]
                    for k in range(KC):
                        last = nc.vector.tensor_tensor(M[:, k].rearrange("p b s -> p (b s)"), Mraw[:, k], mean,
                                                       ALU.subtract)
                    last.then_inc(pro_c, 1)

            def block_scales(m):
                dve.wait_ge(wn_ld[m], 16)
                linked(nc.vector.tensor_reduce(bmax, WN.rearrange("p (n e) -> p n e", e=BLK), AX.X, ALU.max,
                                               apply_absolute_value=True))
                scalar2(bscl, bmax, 1.0 / 7.0, TINY, ALU.mult, ALU.max)
                linked(nc.vector.reciprocal(binv, bscl))
                nc.vector.tensor_reduce(col[f"wmx{m}"], bscl, AX.X, ALU.max).then_inc(col_max, 1)

            def common_scale(m, k):
                dve.wait_ge(col_all, k + 1)
                linked(nc.vector.tensor_scalar(col["rpw"].bitcast(I32), col[f"wall{m}"].bitcast(I32), 0x7F800000, None,
                                               ALU.bitwise_and))
                scalar2(col[f"pw{m}"], col["rpw"], 1.0 / WTOP, 1.0)
                linked(nc.vector.reciprocal(col["rpw"], col[f"pw{m}"]))
                nc.vector.tensor_scalar(bscl, bscl, col["rpw"], None, ALU.mult).then_inc(w_blk, 1)

            block_scales(0)
            common_scale(0, 0)

            def score_max(g):
                c = bass.ds(TI * g, TI)
                dve.wait_ge(sc_mm, g + 1)
                nc.vector.tensor_reduce(smax[:, c], ps[:, 2].rearrange("p (i s) -> p i s", i=TI), AX.X,
                                        ALU.max).then_inc(smax_d, 1)
                dve.wait_ge(smax_d, g + 1)
                dve.wait_ge(rs1_d, 2 * g + 2)
                nc.vector.scalar_tensor_tensor(nmax[:, c], smax[:, c], -1.0, rs1[:, c], ALU.mult,
                                               ALU.mult).then_inc(nmax_d, 1)

            def residual(g):
                c = bass.ds(TI * g, TI)
                dve.wait_ge(exp_d, TI * g + TI)
                nc.vector.reciprocal(rinv[:, c], rsum[:, c]).then_inc(rinv_d, 1)
                dve.wait_ge(rinv_d, g + 1)

                def stats(i):
                    dve.wait_ge(x2_d_s, TI * g + i + 1)
                    nc.vector.bn_stats(bn[:, i], X[:, g, i]).then_inc(bn2_d, 1)

                for i in range(TI):
                    dve.wait_ge(av_mm, TI * g + i + 1)
                    nc.vector.scalar_tensor_tensor(X[:, g, i], ps[:, 4 + i % 2], rinv[:, bass.ds(TI * g + i, 1)],
                                                   X[:, g, i], ALU.mult, ALU.add).then_inc(x2_d_s, 1)
                    if i:
                        stats(i - 1)
                stats(TI - 1)
                for i in range(TI):
                    dve.wait_ge(bn2_d, TI * g + i + 1)
                    nc.vector.bn_aggr(mv[:, i], bn[:, i]).then_inc(mv2_d, 1)
                dve.wait_ge(mv2_d, TI * g + TI)
                nc.vector.tensor_scalar(negm[:, c], mv[:, 0:TI, 0], -1.0, None, ALU.mult)
                nc.vector.tensor_scalar(ve[:, c], mv[:, 0:TI, 1], EPS, None, ALU.add).then_inc(ve2_d, 1)

            def h_max(g):
                dve.wait_ge(ht_ev, TI * g + TI)
                nc.vector.tensor_reduce(hcol[:, bass.ds(g, 1)], HT[:, g].rearrange("p k t -> p (k t)"), AX.X, ALU.max,
                                        apply_absolute_value=True).then_inc(hcol_d, 1)

            score_max(0)
            score_max(1)
            residual(0)
            for g in range(2, NG):
                score_max(g)
                residual(g - 1)
                h_max(g - 2)
            residual(NG - 1)
            h_max(NG - 2)

            def weights_lo(m, c, bank):
                dve.wait_ge(wt_hi, m * OC + c + 1)
                src = ps[:, bank]
                if m == 2:
                    hi, lo = wd_prep[:, 0, c], wd_prep[:, 1, c]
                else:
                    hi, lo = ((WG, WU)[m][:, l, :, c * P:(c + 1) * P] for l in range(2))
                    src = src.rearrange("p (k o) -> p k o", k=KC)
                nc.vector.tensor_tensor(lo, src, hi, ALU.subtract).then_inc(wt_lo, 1)

            for c in range(OC):
                weights_lo(0, c, c % 3)
            h_max(NG - 1)

            def quant_scale(scale, inv, tmp, rec, whole, factor):
                scalar2(col[tmp], col[whole], factor, 1.0 / QMAX)
                scalar2(col[scale], col[tmp], TINY, None, ALU.max, ALU.bypass)
                linked(nc.vector.reciprocal(col[rec], col[scale]))
                return nc.vector.tensor_scalar(col[inv], col[rec], factor, None, ALU.mult)

            dve.wait_ge(hcol_d, NG)
            nc.vector.tensor_reduce(col["hmx"], hcol, AX.X, ALU.max).then_inc(col_max, 1)
            dve.wait_ge(col_all, 2)
            quant_scale("xs", "xinv", "gt", "grc", "hall", 1.0).then_inc(xinv_d, 1)
            dve.wait_ge(x2_st, 16 * NG)
            for g in range(NG):
                dve.wait_ge(hq_d, g + 1)
                nc.vector.tensor_copy(XT[:, g, 0].rearrange("p k t -> p (k t)"), hq[:, g % 2]).then_inc(hhi_d, 1)
                dve.wait_ge(hhi_d, g + 1)
                nc.vector.tensor_tensor(XT[:, g, 1].rearrange("p k t -> p (k t)"), hq[:, g % 2],
                                        XT[:, g, 0].rearrange("p k t -> p (k t)"), ALU.subtract).then_inc(hlo_d, 1)
            scalar2(col["fg"], col["xs"], col["pw0"], 1.0)

            def gate_max(g, turned=None):
                for n in range(UPG):
                    dve.wait_ge(g_ev, g * UPG + n + 1)
                    nc.vector.tensor_reduce(gcol[:, bass.ds(g * UPG + n, 1)], gate_out[:, n % 2], AX.X, ALU.max,
                                            apply_absolute_value=True).then_inc(g_mx, 1)
                    if turned is not None:
                        for c in (2 * n, 2 * n + 1):
                            weights_lo(turned, c, 4 + c % 4)

            block_scales(1)
            common_scale(1, 2)
            gate_max(0)
            with nc.vector.Fori(1, 3) as g:
                gate_max(g)
            gate_max(3, 1)
            gate_max(4)
            block_scales(2)
            common_scale(2, 3)
            with nc.vector.Fori(5, 7) as g:
                gate_max(g)
            gate_max(7, 2)
            dve.wait_ge(g_mx, NU)
            nc.vector.tensor_reduce(col["gmx"], gcol, AX.X, ALU.max).then_inc(col_max, 1)
            dve.wait_ge(col_all, 5)
            quant_scale("gsc", "ginv", "gt", "grc", "gall", col["fg"]).then_inc(ginv_d, 1)
            scalar2(col["fu"], col["xs"], col["pw1"], 1.0)

            def up_max(n, s):
                dve.wait_ge(u_ev, n + 1)
                nc.vector.tensor_reduce(ucol[:, bass.ds(n, 1)], up_out[:, s], AX.X, ALU.max,
                                        apply_absolute_value=True).then_inc(u_mx, 1)

            def round_sig(v, s, first, base):
                dve.wait_ge(sig_d, base + v + 1)
                if not first:
                    dve.wait_ge(a_mx if base == 0 else b_d, v)
                nc.vector.tensor_scalar(sigq, gate_in[:, s], 65536.0, 65535.0, ALU.mult, ALU.min).then_inc(r_d, 1)

            def act_max(v, s):
                dve.wait_ge(aq_d, v + 1)
                dve.wait_ge(r_d, v + 1)
                nc.vector.tensor_tensor_reduce(gate_in[:, s], aq[:, s], sigq, 1.0, scol[:, s:s + 1], ALU.mult, ALU.max,
                                               scol[:, s:s + 1]).then_inc(a_mx, 1)

            def act_int(v, s):
                dve.wait_ge(r_d, NU + v + 1)
                nc.vector.scalar_tensor_tensor(Q[:, v], Q[:, v], col["sinv"], sigq, ALU.mult, ALU.mult).then_inc(b_d, 1)

            def slot_a(n, v, s, first):
                round_sig(v, 0, first, 0)
                up_max(n, s)
                act_max(v, 0)
                round_sig(v + 1, 1, False, 0)
                act_max(v + 1, 1)

            def slot_b(n, v, s, first):
                round_sig(v, 0, first, NU)
                up_max(n, s)
                act_int(v, 0)
                round_sig(v + 1, 1, False, NU)
                act_int(v + 1, 1)

            for n in range(NU // 2):
                slot_a(n, 2 * n, n % 2, n == 0)
            dve.wait_ge(a_mx, NU)
            nc.vector.tensor_reduce(col["smx"], scol, AX.X, ALU.max).then_inc(col_max, 1)
            scalar2(col["su"], col["gsc"], 1.0 / 65536.0, 1.0)
            dve.wait_ge(col_all, 6)
            linked(quant_scale("ssc", "sinv", "st", "src", "sall", col["su"]))
            slot_b(24, 0, 0, True)
            slot_b(25, 2, 1, False)
            with nc.vector.Fori(13, 24) as t:
                for s in range(2):
                    slot_b(2 * t + s, 4 * t - 48 + 2 * s, s, False)
            dve.wait_ge(u_mx, NU)
            nc.vector.tensor_reduce(col["umx"], ucol, AX.X, ALU.max).then_inc(col_max, 1)
            dve.wait_ge(col_all, 7)
            quant_scale("usc", "uinv", "ut", "urc", "uall", col["fu"]).then_inc(uinv_d, 1)
            scalar2(col["oo"], col["ssc"], col["usc"], 1.0)

            def o_max(t, k):
                n = 12 * t + k
                if k % 3 == 2:
                    need(dve, o_mx, n - 1)
                    nc.vector.scalar_tensor_tensor(qb[:, k % 2], Q[:, n], -1.0, Q[:, n], ALU.mult,
                                                   ALU.max).then_inc(agv_d, 1)
                    dve.wait_ge(agv_d, 4 * t + k // 3 + 1)
                else:
                    dve.wait_ge(ag_d, 8 * t + 2 * (k // 3) + k % 3 + 1)
                dve.wait_ge(au_d, n + 1)
                nc.vector.tensor_tensor_reduce(ring[:, k % 4], qa[:, k % 2], qb[:, k % 2], 1.0, ocol[:, k:k + 1], ALU.mult,
                                               ALU.max, ocol[:, k:k + 1]).then_inc(o_mx, 1)

            for t in range(4):
                for k in range(12):
                    o_max(t, k)
            dve.wait_ge(o_mx, NU)
            nc.vector.tensor_reduce(col["omx"], ocol, AX.X, ALU.max).then_inc(col_max, 1)
            dve.wait_ge(col_all, 8)
            linked(quant_scale("osc", "oinv", "ot", "orc", "oall", col["oo"]))
            scalar2(col["fin"], col["osc"], col["pw2"], 1.0)

            def o_int(t, k):
                n = 12 * t + k
                s, c = k // UPG, 2 * (k % UPG)
                hi = OT[:, s, 0, c:c + 2].rearrange("p c t -> p (c t)")
                lo = OT[:, s, 1, c:c + 2].rearrange("p c t -> p (c t)")
                if k % UPG == 0:
                    need(dve, dn_mm, 2 * (2 * t + s) - 2)
                dve.wait_ge(uq_d, n + 1)
                nc.vector.scalar_tensor_tensor(qb[:, k % 2], qa[:, k % 2], col["oinv"], Q[:, n], ALU.mult,
                                               ALU.mult).then_inc(oq_d, 1)
                dve.wait_ge(oq_d, n + 1)
                nc.vector.tensor_copy(hi, qb[:, k % 2]).then_inc(ohi_d, 1)
                dve.wait_ge(ohi_d, n + 1)
                nc.vector.tensor_tensor(lo, qb[:, k % 2], hi, ALU.subtract).then_inc(olo_d, 1)

            def finish(g, s):
                for r in range(2):
                    dve.wait_ge(dn_mm, 2 * g + r + 1)
                    dve.wait_ge(x2_ld[r], 16 * g + 16)
                    nc.vector.scalar_tensor_tensor(x2_in[:, r], ps[:, 4 * s + 2 * r:4 * s + 2 * r + 2].rearrange("p b w -> p (b w)"),
                                                   col["fin"], x2_in[:, r], ALU.mult, ALU.add).then_inc(fin_d, 1)

            for k in range(UPG):
                o_int(0, k)
            for k in range(UPG, 2 * UPG):
                o_int(0, k)
            finish(0, 0)
            with nc.vector.Fori(1, 4) as t:
                for k in range(UPG):
                    o_int(t, k)
                finish(2 * t - 1, 1)
                for k in range(UPG, 2 * UPG):
                    o_int(t, k)
                finish(2 * t, 0)
            finish(NG - 1, 1)


_INS = ['x', 'ctx_1024', 'L0_xattn_Wq', 'L0_xattn_Wkv', 'L0_ffn_w_gate', 'L0_ffn_w_up', 'L0_ffn_w_down']
_OUTS = [((B, S, D), 'float32')]


def kernel(**inputs):
    import numpy as _np
    import concourse.bacc as _bacc
    from concourse import mybir as _mybir
    from concourse.bass_utils import run_bass_kernel_spmd as _run

    nc = _bacc.Bacc("TRN2", target_bir_lowering=False, num_devices=1)
    arrays, args = {}, []
    for name in _INS:
        a = _np.ascontiguousarray(inputs[name])
        arrays[f"in_{name}_dram"] = a
        args.append(nc.dram_tensor(f"in_{name}_dram", a.shape, _mybir.dt.from_np(a.dtype), kind="ExternalInput").ap())
    for i, (shape, dtype) in enumerate(_OUTS):
        dt = _mybir.dt.from_np(_np.dtype(dtype))
        args.append(nc.dram_tensor(f"out_{i}_dram", shape, dt, kind="ExternalOutput").ap())
    build(nc, *args)
    r = _run(nc, [arrays], core_ids=[0])
    got = tuple(r.results[0][f"out_{i}_dram"] for i in range(len(_OUTS)))
    return got[0]
```

```python
from contextlib import ExitStack

import concourse.bass as bass
from concourse import mybir

P = 128
B, S, D = 2, 2048, 512
KV = 128
I = 1536
T = B * S
EPS = 1e-5
QMAX = 32767.0
TINY = 1e-12
BLK = 32
NG = T // 512
TI = 4
KC = D // P
OC = I // P
UPG = OC // 2
NU = NG * UPG
GPB = NG // B
UW = 1024
NBLK = OC * D // BLK
SCALE = float(D) ** -0.5
ROUND = 12582912.0
PV_LAG = TI + 3
X2_LAG = PV_LAG + 1
H_LAG = X2_LAG + TI + 3
WTOP = 2048.0

F32 = mybir.dt.float32
F16 = mybir.dt.float16
I16 = mybir.dt.int16
U16 = mybir.dt.uint16
I32 = mybir.dt.int32
ALU = mybir.AluOpType
ACT = mybir.ActivationFunctionType
AX = mybir.AxisListType
RMAX = bass.bass_isa.ReduceOp.max


def need(eng, sem, value):
    if isinstance(value, int) and value <= 0:
        return
    eng.wait_ge(sem, value)


def build(nc, x, ctx_in, wq_in, wkv_in, wg_in, wu_in, wd_in, out):
    x_v = x.rearrange("b (p j i) d -> b j p (i d)", p=P, j=GPB, i=TI)
    out_v = out.rearrange("b (p j i) d -> b j p (i d)", p=P, j=GPB, i=TI)
    gate_d = nc.dram_tensor("gate_park", [NU, P, UW], F32).ap()
    up_d = nc.dram_tensor("up_park", [NU, P, UW], F32).ap()
    x2_d = nc.dram_tensor("x2_park", [NG, P, TI * D], F32).ap()
    wd_d = nc.dram_tensor("wdown_park", [P, 12288], F16).ap()

    with ExitStack() as stack:
        def sem(name):
            return stack.enter_context(nc.semaphore(name))

        big = stack.enter_context(nc.sbuf_tensor("big", [P, 51200], F32))
        small = stack.enter_context(nc.sbuf_tensor("small", [P, 1840], F32))
        ps = stack.enter_context(nc.psum_tensor("ps", [P, 8, 512], F32))

        def part(start, words):
            return big[:, start:start + words]

        def cut(start, words):
            return small[:, start:start + words]

        X = part(0, 16384).rearrange("p (g i d) -> p g i d", g=NG, i=TI)
        XT = part(0, 16384).bitcast(F16).rearrange("p (g l k t) -> p g l k t", g=NG, l=2, k=KC)
        OT = part(0, 12288).bitcast(F16).rearrange("p (s l c t) -> p s l c t", s=2, l=2, c=OC)
        ring6 = part(12288, 4096).rearrange("p (s w) -> p s w", s=4)
        ring5 = part(4096, 6144).rearrange("p (s w) -> p s w", s=6)
        HT0 = 16384
        HT = part(HT0, 16384).rearrange("p (g k t) -> p g k t", g=NG, k=KC)
        cmean = part(HT0 + 2048, 128)
        ctx_sb = part(HT0 + 4096, 1024).rearrange("p (b d) -> p b d", b=B)
        ctxT = part(HT0 + 5120, 1024).rearrange("p (k b s) -> p k b s", k=KC, b=B)
        KT = part(HT0 + 6144, 1024).rearrange("p (k s) -> p k s", k=KC)
        Mraw = part(HT0 + 7168, 1024).rearrange("p (k s) -> p k s", k=KC)
        wkv = part(HT0 + 8192, 4096).rearrange("p (k n) -> p k n", k=KC)
        wqT = part(HT0 + 12288, 2048).rearrange("p (k n) -> p k n", k=KC)
        wq = part(HT0 + 14336, 2048).rearrange("p (k n) -> p k n", k=KC)
        gate_out = part(HT0, 2048).rearrange("p (s w) -> p s w", s=2)
        wd_prep = part(HT0 + 2048, 6144).bitcast(F16).rearrange("p (l c n) -> p l c n", l=2, c=OC)
        WG = part(32768, 6144).bitcast(F16).rearrange("p (l k o) -> p l k o", l=2, k=KC)
        WN = part(38912, 6144)
        U0 = 45056
        WU = part(U0, 6144).bitcast(F16).rearrange("p (l k o) -> p l k o", l=2, k=KC)
        WD = part(U0, 6144).bitcast(F16).rearrange("p (l c n) -> p l c n", l=2, c=OC)
        M = part(U0, 1024).rearrange("p (k b s) -> p k b s", k=KC, b=B)
        V = part(U0 + 1024, 1024).rearrange("p (b d) -> p b d", b=B)
        xTs = part(U0 + 2048, 1024).rearrange("p (s k t) -> p s k t", s=2, k=KC)
        Pe = part(U0 + 3072, 512).rearrange("p (i s) -> p i s", i=TI)
        PTs = part(U0 + 3584, 512).rearrange("p (i t) -> p i t", i=TI)
        h2 = part(U0 + 4096, 2048).rearrange("p (s d) -> p s d", s=4)
        hq = part(U0, 2048).bitcast(I16).rearrange("p (s w) -> p s w", s=2)
        Q = part(HT0, 24576).bitcast(I16).rearrange("p (u w) -> p u w", u=NU)
        up_out = part(40960, 2048).rearrange("p (s w) -> p s w", s=2)
        AHEAD = 4
        sweep_own = part(43008, 2048).rearrange("p (s w) -> p s w", s=2)
        sweep_early = part(36864, 4096).rearrange("p (s w) -> p s w", s=4)
        sweep_late = part(0, 4096).rearrange("p (s w) -> p s w", s=4)

        def gate_in(j, late):
            return sweep_own[:, j] if j < 2 else (sweep_late if late else sweep_early)[:, j - 2]

        qa5 = part(40960, 2048).bitcast(I16).rearrange("p (s w) -> p s w", s=4)
        qb5 = part(43008, 2048).bitcast(I16).rearrange("p (s w) -> p s w", s=4)
        qa = part(40960, 1024).bitcast(I16).rearrange("p (s w) -> p s w", s=2)
        qb = part(41984, 1024).bitcast(I16).rearrange("p (s w) -> p s w", s=2)
        x2_in = part(43008, 2048).rearrange("p (s w) -> p s w", s=2)

        bn = cut(0, 192).rearrange("p (n s) -> p n s", n=32)
        ve = cut(256, 32)
        rs1 = cut(288, 32)
        nmax = cut(320, 32)
        rsum = cut(352, 32)
        rinv = cut(384, 32)
        negm = cut(416, 32)
        xsum = cut(192, 32)
        ssq = cut(224, 32)
        rs2 = cut(448, 32)
        ve1 = cut(1504, 32)
        smax = cut(480, 32)
        mv = cut(1800, 16).rearrange("p (n s) -> p n s", n=8)
        half = cut(512, 32)
        bmax = cut(544, 192)
        binv = cut(736, 192)
        bscl = cut(928, 192)
        ident = cut(1120, 128)
        squares = cut(1248, 256).bitcast(mybir.dt.bfloat16)
        aq = cut(0, 1024).bitcast(I16).rearrange("p (s w) -> p s w", s=2)
        sigq = cut(1024, 512).bitcast(U16)
        hcol = cut(1544, 32)
        gcol = cut(1544, 48)
        ucol = cut(1592, 48)
        scol = cut(1640, 2)
        ocol = cut(1688, 12)
        sc = cut(1736, 64)

        names = ("hmx hall gmx gall umx uall smx sall omx oall wmx0 wall0 wmx1 wall1 wmx2 wall2 "
                 "pw0 pw1 pw2 rpw xs xinv fg gt gsc grc ginv fu usc uinv ut urc st ssc sinv src su ot osc "
                 "oinv orc oo fin0 fin").split()
        col = {n: sc[:, k:k + 1] for k, n in enumerate(names)}

        x_ld = [sem(f"x_ld{g}") for g in range(NG)]
        ctx_ld, wq_ld, wk_ld, wv_ld = sem("ctx_ld"), sem("wq_ld"), sem("wk_ld"), sem("wv_ld")
        wn_ld = [sem(f"wn_ld{m}") for m in range(3)]
        consts = sem("consts")
        pro_mm, pro_ev, pro_c = sem("pro_mm"), sem("pro_ev"), sem("pro_c")
        ve1_d, rs1_d = sem("ve1_d"), sem("rs1_d")
        xt_mm, xt_ev, sc_mm, nmax_d, exp_d = sem("xt_mm"), sem("xt_ev"), sem("sc_mm"), sem("nmax_d"), sem("exp_d")
        smax_d, rinv_d = sem("smax_d"), sem("rinv_d")
        pt_mm, pt_ev, av_mm, x2_d_s = sem("pt_mm"), sem("pt_ev"), sem("av_mm"), sem("x2_done")
        bn1_d, mv1_d, negm_d, ssq_d, ve2_d, rs2_d, h2_d = (sem(n) for n in
                                                           ("bn1_d", "mv1_d", "negm_d", "ssq_d", "ve2_d", "rs2_d", "h2_d"))
        ht_mm, ht_ev, hcol_d, x2_st = sem("ht_mm"), sem("ht_ev"), sem("hcol_d"), sem("x2_st")
        w_blk, w_inv, w_rnd, w_deq = sem("w_blk"), sem("w_inv"), sem("w_rnd"), sem("w_deq")
        wt_mm, wt_hi, wt_lo, wd_st, wd_ld = sem("wt_mm"), sem("wt_hi"), sem("wt_lo"), sem("wd_st"), sem("wd_ld")
        link = sem("link")
        col_max, col_all = sem("col_max"), sem("col_all")
        xinv_d, hq_d, hhi_d, hlo_d = sem("xinv_d"), sem("hq_d"), sem("hhi_d"), sem("hlo_d")
        g_mm, g_ev, g_mx = sem("g_mm"), sem("g_ev"), sem("g_mx")
        g_st = [sem("g_st0"), sem("g_st1")]
        u_mm, u_ev, u_mx = sem("u_mm"), sem("u_ev"), sem("u_mx")
        u_st = [sem("u_st0"), sem("u_st1")]
        g_ld = [sem(f"g_ld{j}") for j in range(6)]
        ginv_d, q_d, aq_d, sig_d, r_d, a_mx, b_d = (sem(n) for n in
                                                  ("ginv_d", "q_d", "aq_d", "sig_d", "r_d", "a_mx", "b_d"))
        uinv_d, au_d, ag_d, agv_d, o_mx = (sem(n) for n in ("uinv_d", "au_d", "ag_d", "agv_d", "o_mx"))
        r5_ld = [sem(f"r5_ld{s}") for s in range(6)]
        r6_ld = [sem(f"r6_ld{s}") for s in range(4)]
        uq_d, oq_d, ohi_d, olo_d = sem("uq_d"), sem("oq_d"), sem("ohi_d"), sem("olo_d")
        dn_mm, fin_d = sem("dn_mm"), sem("fin_d")
        x2_ld = [sem("x2_ld0"), sem("x2_ld1")]
        out_st = [sem("out_st0"), sem("out_st1")]

        block = stack.enter_context(nc.Block())

        def batch(g):
            return g // GPB

        @block.sync
        def _(sp):
            sp.dma_start(ctx_sb, ctx_in.rearrange("b s d -> s b d")).then_inc(ctx_ld, 16)
            sp.dma_start(wq, wq_in.rearrange("(k p) n -> p k n", p=P)).then_inc(wq_ld, 16)
            sp.dma_start(wkv[:, :, 0:D], wkv_in.rearrange("(k p) n -> p k n", p=P)[:, :, 0:D]).then_inc(wk_ld, 16)
            for g in range(NG):
                sp.dma_start(X[:, g].rearrange("p i d -> p (i d)"), x_v[g // GPB, g % GPB]).then_inc(x_ld[g], 16)
                if g == 0:
                    sp.dma_start(wkv[:, :, D:2 * D],
                                 wkv_in.rearrange("(k p) n -> p k n", p=P)[:, :, D:2 * D]).then_inc(wv_ld, 16)
                if g == 2:
                    sp.dma_start(WN.rearrange("p (c d) -> p c d", c=OC),
                                 wg_in.rearrange("(c p) d -> p c d", p=P)).then_inc(wn_ld[0], 16)
            with nc.sync.Fori(0, NG) as g:
                sp.wait_ge(x2_d_s, TI * g + TI)
                sp.dma_start(x2_d[g], X[:, g].rearrange("p i d -> p (i d)")).then_inc(x2_st, 16)
            sp.wait_ge(wt_lo, OC)
            sp.dma_start(WN.rearrange("p (c d) -> p c d", c=OC),
                         wu_in.rearrange("(c p) d -> p c d", p=P)).then_inc(wn_ld[1], 16)

            def park_gate(g):
                for n in range(UPG):
                    sp.wait_ge(g_ev, g * UPG + n + 1)
                    sp.dma_start(gate_d[g * UPG + n], gate_out[:, n % 2]).then_inc(g_st[n % 2], 16)

            with nc.sync.Fori(0, 4) as g:
                park_gate(g)
            sp.wait_ge(wt_lo, 2 * OC)
            sp.dma_start(WN.rearrange("p (h n) -> p h n", h=KC),
                         wd_in.rearrange("(h p) n -> p h n", p=P)).then_inc(wn_ld[2], 16)
            with nc.sync.Fori(4, NG) as g:
                park_gate(g)
            sp.wait_ge(wt_lo, 3 * OC)
            sp.dma_start(wd_d, wd_prep.rearrange("p l c n -> p (l c n)")).then_inc(wd_st, 16)
            for s in range(2):
                sp.wait_ge(g_st[s], 16 * NU // 2)

            def fetch_gate(v, j, late):
                need(sp, a_mx, v - 5)
                sp.dma_start(gate_in(j, late), gate_d[v]).then_inc(g_ld[j], 16)

            def park_up(n, s):
                sp.wait_ge(u_ev, n + 1)
                sp.dma_start(up_d[n], up_out[:, s]).then_inc(u_st[s], 16)

            def group_a(g, last_late):
                for n in range(UPG):
                    park_up(g * UPG + n, n % 2)
                    for k in (2 * n + AHEAD, 2 * n + AHEAD + 1):
                        fetch_gate(12 * g + k, k % 6, last_late and k >= 12)

            sp.wait_ge(wt_lo, 3 * OC)
            sp.wait_ge(g_mm, NU)
            for v in range(AHEAD):
                fetch_gate(v, v, False)
            group_a(0, False)
            with nc.sync.Fori(1, 2) as g:
                group_a(g, False)
            group_a(2, True)
            for n in range(UPG):
                park_up(3 * UPG + n, n % 2)
                for k in (2 * n + AHEAD, 2 * n + AHEAD + 1):
                    if k < 12:
                        fetch_gate(36 + k, k % 6, True)
            with nc.sync.Fori(4, 6) as g:
                for n in range(UPG):
                    park_up(g * UPG + n, n % 2)
            sp.wait_ge(u_mm, 5 * UPG)
            for k in range(6):
                sp.dma_start(ring5[:, k], up_d[k]).then_inc(r5_ld[k], 16)
            with nc.sync.Fori(6, NG) as g:
                for n in range(UPG):
                    park_up(g * UPG + n, n % 2)
            sp.wait_ge(wd_st, 16)
            sp.wait_ge(u_mm, NU)
            sp.dma_start(WD.rearrange("p l c n -> p (l c n)"), wd_d).then_inc(wd_ld, 16)
            for s in range(4):
                sp.dma_start(ring6[:, s], up_d[s]).then_inc(r6_ld[s], 16)
            for s in range(2):
                sp.wait_ge(u_st[s], 16 * NU // 2)
            with nc.sync.Fori(1, NU // 6) as t:
                for s in range(6):
                    sp.wait_ge(o_mx, 6 * t + s - 5)
                    sp.dma_start(ring5[:, s], up_d[6 * t + s]).then_inc(r5_ld[s], 16)
            sp.wait_ge(x2_st, 16 * NG)
            sp.wait_ge(o_mx, NU)

            def fetch_x2(g, r):
                sp.dma_start(x2_in[:, r], x2_d[g, :, r * UW:(r + 1) * UW]).then_inc(x2_ld[r], 16)

            def store_out(b, j, g, r):
                sp.wait_ge(fin_d, 2 * g + r + 1)
                sp.dma_start(out_v[b, j, :, r * UW:(r + 1) * UW], x2_in[:, r]).then_inc(out_st[r], 16)

            def fetch_up(n, s):
                sp.wait_ge(uq_d, n - 3)
                sp.dma_start(ring6[:, s], up_d[n]).then_inc(r6_ld[s], 16)

            for r in range(2):
                fetch_x2(0, r)
            for n in range(4, 2 * UPG):
                fetch_up(n, n % 4)
            for s in range(2):
                for n in range(UPG):
                    fetch_up((s + 2) * UPG + n, (s * UPG + n) % 4)
                for r in range(2):
                    store_out(0, s, s, r)
                for r in range(2):
                    sp.wait_ge(out_st[r], 16 * (s + 1))
                    fetch_x2(s + 1, r)
            with nc.sync.Fori(1, 3) as t:
                for s in range(2):
                    g = 2 * t + s
                    for n in range(UPG):
                        fetch_up((g + 2) * UPG + n, (s * UPG + n) % 4)
                    for r in range(2):
                        store_out(batch(g), g % GPB, g, r)
                    for r in range(2):
                        sp.wait_ge(out_st[r], 16 * (g + 1))
                        fetch_x2(g + 1, r)
            for g in range(NG - 2, NG):
                for r in range(2):
                    store_out(g // GPB, g % GPB, g, r)
                if g < NG - 1:
                    for r in range(2):
                        sp.wait_ge(out_st[r], 16 * (g + 1))
                        fetch_x2(g + 1, r)
            for r in range(2):
                sp.wait_ge(out_st[r], 16 * NG)

        @block.gpsimd
        def _(pool):
            nc.gpsimd.memset(ident, 0.0).then_inc(consts, 1)
            nc.gpsimd.memset(half, -0.5).then_inc(consts, 1)
            nc.gpsimd.memset(cmean, 1.0 / D).then_inc(consts, 1)
            pool.wait_ge(consts, 1)
            nc.gpsimd.affine_select(out=ident, in_=ident, compare_op=ALU.not_equal, fill=1.0, base=0,
                                    pattern=[[-1, P]], channel_multiplier=1).then_inc(consts, 1)
            pool.wait_ge(consts, 4)
            def rstd1(g):
                r = rs1[:, TI * g:TI * g + TI]
                pool.wait_ge(ve1_d, g + 1)
                nc.gpsimd.tensor_tensor(r, ve1[:, TI * g:TI * g + TI], half[:, TI * g:TI * g + TI],
                                        ALU.pow).then_inc(rs1_d, 1)
                pool.wait_ge(rs1_d, 2 * g + 1)
                nc.gpsimd.tensor_scalar(r, r, SCALE, 1.0, ALU.mult, ALU.mult).then_inc(rs1_d, 1)

            for g in range(3):
                rstd1(g)

            def all_max(k, src, dst):
                pool.wait_ge(col_max, k + 1)
                nc.gpsimd.partition_all_reduce(col[dst], col[src], P, RMAX).then_inc(col_all, 1)

            def quant_weights(at, blocks, base):
                w = WN[:, bass.ds(at * blocks * BLK, blocks * BLK)]
                wb = w.rearrange("p (n e) -> p n e", e=BLK)
                inv = binv[:, bass.ds(at * blocks, blocks)].unsqueeze(2).to_broadcast([P, blocks, BLK])
                scl = bscl[:, bass.ds(at * blocks, blocks)].unsqueeze(2).to_broadcast([P, blocks, BLK])
                nc.gpsimd.tensor_tensor(wb, wb, inv, ALU.mult).then_inc(w_inv, 1)
                pool.wait_ge(w_inv, base + at + 1)
                nc.gpsimd.tensor_scalar(w, w, ROUND, 1.0, ALU.add, ALU.mult).then_inc(w_rnd, 1)
                pool.wait_ge(w_rnd, 2 * base + 2 * at + 1)
                nc.gpsimd.tensor_scalar(w, w, -ROUND, 1.0, ALU.add, ALU.mult).then_inc(w_rnd, 1)
                pool.wait_ge(w_rnd, 2 * base + 2 * at + 2)
                nc.gpsimd.tensor_tensor(wb, wb, scl, ALU.mult).then_inc(w_deq, 1)

            def normalise(g):
                c = bass.ds(TI * g, TI)
                pool.wait_ge(ve2_d, g + 1)
                nc.gpsimd.tensor_tensor(rs2[:, c], ve[:, c], half[:, c], ALU.pow).then_inc(rs2_d, 1)
                pool.wait_ge(rs2_d, g + 1)
                for i in range(TI):
                    need(pool, ht_mm, TI * g + i - 3)
                    nc.gpsimd.tensor_scalar(h2[:, i], X[:, g, i], negm[:, bass.ds(TI * g + i, 1)],
                                            rs2[:, bass.ds(TI * g + i, 1)], ALU.add, ALU.mult).then_inc(h2_d, 1)

            all_max(0, "wmx0", "wall0")
            pool.wait_ge(w_blk, 1)
            for at in range(3):
                quant_weights(at, NBLK // 8, 0)
            rstd1(3)
            for g in range(NG):
                normalise(g)
                if g < 4:
                    rstd1(g + 4)
                if g < 5:
                    quant_weights(g + 3, NBLK // 8, 0)
            all_max(1, "hmx", "hall")
            all_max(2, "wmx1", "wall1")
            pool.wait_ge(w_blk, 2)
            quant_weights(0, NBLK, 8)
            all_max(3, "wmx2", "wall2")
            pool.wait_ge(w_blk, 3)
            quant_weights(0, NBLK, 9)
            all_max(4, "gmx", "gall")
            pool.wait_ge(ginv_d, 1)
            pool.wait_ge(wd_st, 16)
            for s in range(2):
                pool.wait_ge(g_st[s], 16 * NU // 2)

            def gate_int(v):
                pool.wait_ge(g_ld[v % 6], 16 * (v // 6) + 16)
                if v >= 40:
                    pool.wait_ge(a_mx, 36)
                nc.gpsimd.tensor_scalar(Q[:, v], gate_in(v % 6, v >= 36), col["ginv"], 1.0,
                                        ALU.mult, ALU.mult).then_inc(q_d, 1)

            for v in range(NU):
                gate_int(v)
            all_max(5, "smx", "sall")
            all_max(6, "umx", "uall")
            all_max(7, "omx", "oall")

        @block.tensor
        def _(pe):
            def turn(dst, src):
                return nc.tensor.transpose(dst, src, ident)

            pe.wait_ge(consts, 4)
            pe.wait_ge(ctx_ld, 16)
            for b in range(B):
                for k in range(KC):
                    mm = turn(ps[:, b, k * P:(k + 1) * P], ctx_sb[:, b, k * P:(k + 1) * P])
                mm.then_inc(pro_mm, 1)
            pe.wait_ge(wq_ld, 16)
            for k in range(KC):
                for m in range(KC):
                    mm = turn(ps[:, 4 + k, m * P:(m + 1) * P], wq[:, k, m * P:(m + 1) * P])
                mm.then_inc(pro_mm, 1)
            pe.wait_ge(wk_ld, 16)
            pe.wait_ge(pro_ev, 2)
            for m in range(KC):
                for k in range(KC):
                    mm = nc.tensor.matmul(ps[:, 2 + m // 2, (m % 2) * 256:(m % 2) * 256 + 256],
                                          wkv[:, k, m * P:(m + 1) * P],
                                          ctxT[:, k].rearrange("p b s -> p (b s)"), start=(k == 0), stop=(k == KC - 1))
                if m % 2:
                    mm.then_inc(pro_mm, 1)
            pe.wait_ge(pro_ev, 8)
            for h in range(KC):
                for m in range(KC):
                    mm = nc.tensor.matmul(ps[:, 6 + h // 2, (h % 2) * 256:(h % 2) * 256 + 256],
                                          wqT[:, m, h * P:(h + 1) * P], KT[:, m],
                                          start=(m == 0), stop=(m == KC - 1))
                if h % 2:
                    mm.then_inc(pro_mm, 1)
            pe.wait_ge(pro_ev, 10)
            for k in range(KC):
                mm = nc.tensor.matmul(ps[:, 2, 0:256], cmean, Mraw[:, k], start=(k == 0), stop=(k == KC - 1))
            mm.then_inc(pro_mm, 1)
            pe.wait_ge(wv_ld, 16)
            for b in range(B):
                for k in range(KC):
                    mm = nc.tensor.matmul(ps[:, 4 + b], ctxT[:, k, b], wkv[:, k, D:2 * D],
                                          start=(k == 0), stop=(k == KC - 1))
                mm.then_inc(pro_mm, 1)
            pe.wait_ge(pro_c, 1)
            pe.wait_ge(pro_ev, 12)

            NT = NG * TI

            def turn_x(n):
                need(pe, xt_ev, n - 1)
                for k in range(KC):
                    mm = turn(ps[:, n % 2, k * P:(k + 1) * P], X[:, n // TI, n % TI, k * P:(k + 1) * P])
                mm.then_inc(xt_mm, 1)

            def scores(n):
                g, i = n // TI, n % TI
                if i == 0:
                    need(pe, exp_d, TI * (g - 1))
                pe.wait_ge(xt_ev, n + 1)
                for k in range(KC):
                    mm = nc.tensor.matmul(ps[:, 2 + g % 2, i * P:(i + 1) * P], xTs[:, n % 2, k], M[:, k, batch(g)],
                                          start=(k == 0), stop=(k == KC - 1))
                mm.then_inc(sc_mm, 1)

            def turn_p(g):
                need(pe, pt_ev, g)
                for i in range(TI):
                    pe.wait_ge(exp_d, TI * g + i + 1)
                    mm = turn(ps[:, 4, i * P:(i + 1) * P], Pe[:, i])
                mm.then_inc(pt_mm, 1)

            def attend(n):
                pe.wait_ge(pt_ev, n // TI + 1)
                need(pe, x2_d_s, n - 1)
                nc.tensor.matmul(ps[:, 5 + n % 2], PTs[:, n % TI], V[:, batch(n // TI)],
                                 start=True, stop=True).then_inc(av_mm, 1)

            def turn_h(n):
                need(pe, ht_ev, n)
                pe.wait_ge(h2_d, n + 1)
                for k in range(KC):
                    mm = turn(ps[:, 7, k * P:(k + 1) * P], h2[:, n % 4, k * P:(k + 1) * P])
                mm.then_inc(ht_mm, 1)

            def turn_weights(m, c, bank, gap):
                if c == 0:
                    pe.wait_ge(w_deq, 8 + m)
                if c >= gap:
                    pe.wait_ge(wt_lo, m * OC + c - gap + 1)
                for k in range(KC):
                    at = k * I + c * P if m == 2 else c * D + k * P
                    mm = turn(ps[:, bank, k * P:(k + 1) * P], WN[:, at:at + P])
                mm.then_inc(wt_mm, 1)

            turn_x(0)
            for n in range(NT + H_LAG):
                if n + 1 < NT:
                    turn_x(n + 1)
                if n < NT:
                    scores(n)
                if PV_LAG <= n < NT + PV_LAG:
                    attend(n - PV_LAG)
                if NT <= n < NT + OC:
                    if n == NT:
                        pe.wait_ge(xt_ev, NT)
                    if n == NT + 3:
                        pe.wait_ge(exp_d, NT)
                    turn_weights(0, n - NT, n % 4, 4)
                if n % TI == 2 and TI <= n < NT + TI:
                    turn_p(n // TI - 1)
                if n >= H_LAG:
                    turn_h(n - H_LAG)

            def unit(w, g, n, done):
                for j in range(2):
                    o = (2 * n + j) * P
                    for k in range(KC):
                        for a, b in ((0, 0), (1, 0), (0, 1)):
                            mm = nc.tensor.matmul(ps[:, 2 * (n % 2) + j], w[:, a, k, o:o + P], XT[:, g, b, k],
                                                  start=(k == 0 and a + b == 0), stop=(k == KC - 1 and b == 1))
                mm.then_inc(done, 1)

            def product(w, g, mm_sem, ev_sem, turned=None):
                for n in range(UPG):
                    need(pe, ev_sem, g * UPG + n - 1)
                    unit(w, g, n, mm_sem)
                    if turned is not None:
                        for c in (2 * n, 2 * n + 1):
                            turn_weights(turned, c, 4 + c % 4, 4)

            def gate(g, turned=None):
                pe.wait_ge(hlo_d, g + 1)
                product(WG, g, g_mm, g_ev, turned)

            pe.wait_ge(wt_lo, OC)
            gate(0)
            with nc.tensor.Fori(1, 3) as g:
                gate(g)
            gate(3, 1)
            with nc.tensor.Fori(4, 7) as g:
                gate(g)
            gate(7, 2)
            pe.wait_ge(wt_lo, 2 * OC)
            pe.wait_ge(g_ev, NU)
            product(WU, 0, u_mm, u_ev)
            with nc.tensor.Fori(1, NG) as g:
                product(WU, g, u_mm, u_ev)

            def down(g, s):
                need(pe, fin_d, 2 * g - 2)
                for n in range(UPG):
                    pe.wait_ge(olo_d, g * UPG + n + 1)
                    for i in range(TI):
                        for c in (2 * n, 2 * n + 1):
                            for a, b in ((0, 0), (0, 1), (1, 0)):
                                mm = nc.tensor.matmul(ps[:, 4 * s + i], OT[:, s, a, c, i * P:(i + 1) * P], WD[:, b, c],
                                                      start=(c == 0 and a + b == 0), stop=(c == OC - 1 and a == 1))
                        if n == UPG - 1 and i % 2:
                            mm.then_inc(dn_mm, 1)

            pe.wait_ge(wd_ld, 16)
            pe.wait_ge(u_ev, NU)
            down(0, 0)
            down(1, 1)
            with nc.tensor.Fori(1, NG // 2) as t:
                for s in range(2):
                    down(2 * t + s, s)

        @block.scalar
        def _(act):
            def copy(dst, src):
                return nc.scalar.activation(dst, src, ACT.Copy)

            for b in range(B):
                act.wait_ge(pro_mm, b + 1)
                copy(ctxT[:, :, b], ps[:, b].rearrange("p (k s) -> p k s", k=KC)).then_inc(pro_ev, 1)
            for k in range(KC):
                act.wait_ge(pro_mm, k + 3)
                copy(wqT[:, :, k * P:(k + 1) * P], ps[:, 4 + k].rearrange("p (m s) -> p m s", m=KC)).then_inc(pro_ev, 1)
            for m in range(2):
                act.wait_ge(pro_mm, m + 7)
                copy(KT[:, 2 * m:2 * m + 2], ps[:, 2 + m].rearrange("p (k s) -> p k s", k=2)).then_inc(pro_ev, 1)
            for m in range(2):
                act.wait_ge(pro_mm, m + 9)
                copy(Mraw[:, 2 * m:2 * m + 2], ps[:, 6 + m].rearrange("p (k s) -> p k s", k=2)).then_inc(pro_ev, 1)
            for b in range(B):
                act.wait_ge(pro_mm, b + 12)
                copy(V[:, b], ps[:, 4 + b]).then_inc(pro_ev, 1)

            NT = NG * TI

            def take_xT(n):
                act.wait_ge(xt_mm, n + 1)
                need(act, sc_mm, n - 1)
                copy(xTs[:, n % 2], ps[:, n % 2].rearrange("p (k t) -> p k t", k=KC)).then_inc(xt_ev, 1)

            def exps(n):
                g, i = n // TI, n % TI
                act.wait_ge(nmax_d, g + 1)
                need(act, pt_mm, g)
                nc.scalar.activation(Pe[:, i], ps[:, 2 + g % 2, i * P:(i + 1) * P], ACT.Exp, bias=nmax[:, n:n + 1],
                                     scale=rs1[:, n:n + 1], accum_out=rsum[:, n:n + 1]).then_inc(exp_d, 1)

            def take_pT(g):
                act.wait_ge(pt_mm, g + 1)
                need(act, av_mm, TI * g)
                copy(PTs, ps[:, 4].rearrange("p (i t) -> p i t", i=TI)).then_inc(pt_ev, 1)

            def spread(n):
                act.wait_ge(negm_d, n + 1)
                need(act, ssq_d, n)
                nc.scalar.activation(squares, X[:, n // TI, n % TI], ACT.Square, bias=negm[:, n:n + 1],
                                     accum_out=ssq[:, n:n + 1]).then_inc(ssq_d, 1)

            def take_hT(n):
                act.wait_ge(ht_mm, n + 1)
                t = (n % TI) * P
                copy(HT[:, n // TI, :, t:t + P], ps[:, 7].rearrange("p (k t) -> p k t", k=KC)).then_inc(ht_ev, 1)

            def weights_hi(m, c, bank):
                act.wait_ge(wt_mm, m * OC + c + 1)
                src = ps[:, bank]
                if m == 2:
                    dst = wd_prep[:, 0, c]
                else:
                    dst = (WG, WU)[m][:, 0, :, c * P:(c + 1) * P]
                    src = src.rearrange("p (k o) -> p k o", k=KC)
                copy(dst, src).then_inc(wt_hi, 1)

            take_xT(0)
            for n in range(NT + H_LAG + 1):
                if n % TI == 3 and TI <= n < NT + TI:
                    take_pT(n // TI - 1)
                if n + 1 < NT:
                    take_xT(n + 1)
                if n > H_LAG:
                    take_hT(n - H_LAG - 1)
                if n % TI == 1 and TI <= n < NT + TI:
                    for i in (2, 3):
                        exps(n - 1 - TI + i)
                if X2_LAG < n <= NT + X2_LAG:
                    spread(n - X2_LAG - 1)
                if NT < n <= NT + OC:
                    weights_hi(0, n - NT - 1, (n - 1) % 4)
                if n % TI == 0 and TI <= n < NT + TI:
                    for i in (0, 1):
                        exps(n - TI + i)

            act.wait_ge(xinv_d, 1)
            for g in range(NG):
                if g >= 2:
                    act.wait_ge(hlo_d, g - 1)
                nc.scalar.activation(hq[:, g % 2], HT[:, g].rearrange("p k t -> p (k t)"), ACT.Copy,
                                     scale=col["xinv"]).then_inc(hq_d, 1)

            def take_gate(g, turned=None):
                for n in range(UPG):
                    act.wait_ge(g_mm, g * UPG + n + 1)
                    need(act, g_mx, g * UPG + n - 1)
                    if not (isinstance(g, int) and g == 0 and n < 2):
                        act.wait_ge(g_st[n % 2], 16 * (g * (UPG // 2) + n // 2))
                    copy(gate_out[:, n % 2], ps[:, 2 * (n % 2):2 * (n % 2) + 2].rearrange("p b w -> p (b w)")).then_inc(g_ev, 1)
                    if turned is not None:
                        for c in (2 * n, 2 * n + 1):
                            weights_hi(turned, c, 4 + c % 4)

            take_gate(0)
            with nc.scalar.Fori(1, 3) as g:
                take_gate(g)
            take_gate(3, 1)
            with nc.scalar.Fori(4, 7) as g:
                take_gate(g)
            take_gate(7, 2)

            def take_up(n, s, first):
                act.wait_ge(u_mm, n + 1)
                if not first:
                    act.wait_ge(u_mx, n - 1)
                    act.wait_ge(u_st[s], 8 * (n - s))
                copy(up_out[:, s], ps[:, 2 * s:2 * s + 2].rearrange("p b w -> p (b w)")).then_inc(u_ev, 1)

            def sweep_a(g, k, late):
                v = 12 * g + k
                act.wait_ge(g_ld[k % 6], 32 * g + 16 * (k // 6) + 16)
                need(act, a_mx, v - 1)
                nc.scalar.activation(aq[:, k % 2], gate_in(k % 6, late), ACT.Abs, scale=col["ginv"]).then_inc(aq_d, 1)

            def sigmoid(g, k, late):
                v = 12 * g + k
                act.wait_ge(q_d, v + 1)
                act.wait_ge(aq_d, v + 1)
                nc.scalar.activation(gate_in(k % 6, late), Q[:, v], ACT.Sigmoid, scale=col["gsc"]).then_inc(sig_d, 1)

            def sweep_b(g, k):
                v = 12 * (g - 4) + k
                if isinstance(g, int) and g == 4 and k < 6:
                    act.wait_ge(a_mx, NU - 5 + k)
                else:
                    act.wait_ge(r_d, NU + v - 5)
                nc.scalar.activation(gate_in(k % 6, True), Q[:, v], ACT.Sigmoid, scale=col["gsc"]).then_inc(sig_d, 1)

            def group_a(g, late=False):
                for n in range(UPG):
                    sweep_a(g, 2 * n, late)
                    sigmoid(g, 2 * n, late)
                    take_up(g * UPG + n + 1, (n + 1) % 2, isinstance(g, int) and g == 0 and n < 1)
                    sweep_a(g, 2 * n + 1, late)
                    sigmoid(g, 2 * n + 1, late)

            def group_b(g):
                for n in range(UPG):
                    sweep_b(g, 2 * n)
                    if not (isinstance(g, int) and g * UPG + n == NU - 1):
                        take_up(g * UPG + n + 1, (n + 1) % 2, False)
                    sweep_b(g, 2 * n + 1)

            act.wait_ge(wt_lo, 3 * OC)
            take_up(0, 0, True)
            act.wait_ge(ginv_d, 1)
            group_a(0)
            with nc.scalar.Fori(1, 3) as g:
                group_a(g)
            group_a(3, True)
            group_b(4)
            with nc.scalar.Fori(5, NG - 1) as g:
                group_b(g)
            group_b(NG - 1)

            act.wait_ge(uinv_d, 1)
            act.wait_ge(b_d, NU)
            for s in range(2):
                act.wait_ge(u_st[s], 16 * NU // 2)

            def magnitudes(t, k):
                s = k % 6
                n = 12 * t + k
                act.wait_ge(r5_ld[s], 16 * (2 * t + k // 6) + 16)
                need(act, o_mx, n - 3)
                nc.scalar.activation(qa5[:, k % 4], ring5[:, s], ACT.Abs, scale=col["uinv"]).then_inc(au_d, 1)
                if k % 3 != 2:
                    nc.scalar.activation(qb5[:, k % 4], Q[:, n], ACT.Abs).then_inc(ag_d, 1)

            for k in range(12):
                magnitudes(0, k)
            with nc.scalar.Fori(1, 4) as t:
                for k in range(12):
                    magnitudes(t, k)

            def up_int(t, k):
                s = k % 4
                n = 12 * t + k
                act.wait_ge(r6_ld[s], 16 * (3 * t + k // 4) + 16)
                need(act, oq_d, n - 1)
                nc.scalar.activation(qa[:, k % 2], ring6[:, s], ACT.Copy, scale=col["uinv"]).then_inc(uq_d, 1)

            act.wait_ge(o_mx, NU)
            for k in range(12):
                up_int(0, k)
            with nc.scalar.Fori(1, 4) as t:
                for k in range(12):
                    up_int(t, k)

        @block.vector
        def _(dve):
            count = [0]

            def linked(ins):
                count[0] += 1
                ins.then_inc(link, 1)
                dve.wait_ge(link, count[0])

            def scalar2(dst, src, s1, s2, op0=ALU.mult, op1=ALU.mult):
                linked(nc.vector.tensor_scalar(dst, src, s1, s2, op0, op1))

            linked(nc.vector.memset(scol, 0.0))
            linked(nc.vector.memset(ocol, 0.0))
            def block_scales(m):
                dve.wait_ge(wn_ld[m], 16)
                linked(nc.vector.tensor_reduce(bmax, WN.rearrange("p (n e) -> p n e", e=BLK), AX.X, ALU.max,
                                               apply_absolute_value=True))
                scalar2(bscl, bmax, 1.0 / 7.0, TINY, ALU.mult, ALU.max)
                linked(nc.vector.reciprocal(binv, bscl))
                nc.vector.tensor_reduce(col[f"wmx{m}"], bscl, AX.X, ALU.max).then_inc(col_max, 1)

            def common_scale(m, k):
                dve.wait_ge(col_all, k + 1)
                linked(nc.vector.tensor_scalar(col["rpw"].bitcast(I32), col[f"wall{m}"].bitcast(I32), 0x7F800000, None,
                                               ALU.bitwise_and))
                scalar2(col[f"pw{m}"], col["rpw"], 1.0 / WTOP, 1.0)
                linked(nc.vector.reciprocal(col["rpw"], col[f"pw{m}"]))
                nc.vector.tensor_scalar(bscl, bscl, col["rpw"], None, ALU.mult).then_inc(w_blk, 1)

            NT = NG * TI

            def stats1(n):
                if n % TI == 0:
                    dve.wait_ge(x_ld[n // TI], 16)
                nc.vector.bn_stats(bn[:, n], X[:, n // TI, n % TI]).then_inc(bn1_d, 1)

            def var1(g):
                dve.wait_ge(bn1_d, TI * g + TI)
                for i in range(TI):
                    nc.vector.bn_aggr(mv[:, i], bn[:, TI * g + i]).then_inc(mv1_d, 1)
                dve.wait_ge(mv1_d, TI * g + TI)
                nc.vector.tensor_scalar(ve1[:, TI * g:TI * g + TI], mv[:, 0:TI, 1], EPS, None,
                                        ALU.add).then_inc(ve1_d, 1)

            def score_max(g):
                c = slice(TI * g, TI * g + TI)
                dve.wait_ge(sc_mm, TI * g + TI)
                nc.vector.tensor_reduce(smax[:, c], ps[:, 2 + g % 2].rearrange("p (i s) -> p i s", i=TI), AX.X,
                                        ALU.max).then_inc(smax_d, 1)
                dve.wait_ge(smax_d, g + 1)
                dve.wait_ge(rs1_d, 2 * g + 2)
                nc.vector.scalar_tensor_tensor(nmax[:, c], smax[:, c], -1.0, rs1[:, c], ALU.mult,
                                               ALU.mult).then_inc(nmax_d, 1)

            def residual(n):
                g, i = n // TI, n % TI
                if i == 0:
                    dve.wait_ge(exp_d, TI * g + TI)
                    nc.vector.reciprocal(rinv[:, n:n + TI], rsum[:, n:n + TI]).then_inc(rinv_d, 1)
                    dve.wait_ge(rinv_d, g + 1)
                dve.wait_ge(av_mm, n + 1)
                nc.vector.scalar_tensor_tensor(X[:, g, i], ps[:, 5 + n % 2], rinv[:, n:n + 1], X[:, g, i],
                                               ALU.mult, ALU.add, accum_out=xsum[:, n:n + 1]).then_inc(x2_d_s, 1)

            def mean2(n):
                dve.wait_ge(x2_d_s, n + 1)
                nc.vector.tensor_scalar(negm[:, n:n + 1], xsum[:, n:n + 1], -1.0 / D, None, ALU.mult).then_inc(negm_d, 1)

            def var2(g):
                c = slice(TI * g, TI * g + TI)
                dve.wait_ge(ssq_d, TI * g + TI)
                nc.vector.tensor_scalar(ve[:, c], ssq[:, c], 1.0 / D, EPS, ALU.mult, ALU.add).then_inc(ve2_d, 1)

            def h_max(n):
                dve.wait_ge(ht_ev, n + 1)
                t = (n % TI) * P
                nc.vector.tensor_reduce(hcol[:, n:n + 1], HT[:, n // TI, :, t:t + P], AX.XY, ALU.max,
                                        apply_absolute_value=True).then_inc(hcol_d, 1)

            def weights_lo(m, c, bank):
                dve.wait_ge(wt_hi, m * OC + c + 1)
                src = ps[:, bank]
                if m == 2:
                    hi, lo = wd_prep[:, 0, c], wd_prep[:, 1, c]
                else:
                    hi, lo = ((WG, WU)[m][:, l, :, c * P:(c + 1) * P] for l in range(2))
                    src = src.rearrange("p (k o) -> p k o", k=KC)
                nc.vector.tensor_tensor(lo, src, hi, ALU.subtract).then_inc(wt_lo, 1)

            for n in range(2 * TI):
                stats1(n)
                if n % TI == TI - 1:
                    var1(n // TI)
            dve.wait_ge(pro_mm, 11)
            dve.wait_ge(pro_ev, 10)
            for k in range(KC):
                last = nc.vector.tensor_tensor(M[:, k].rearrange("p b s -> p (b s)"), Mraw[:, k], ps[:, 2, 0:256],
                                               ALU.subtract)
            last.then_inc(pro_c, 1)
            for n in range(NT + H_LAG + 2):
                if X2_LAG <= n < NT + X2_LAG:
                    residual(n - X2_LAG)
                if n % TI == 0 and TI <= n < NT + TI:
                    score_max(n // TI - 1)
                if n + 2 * TI < NT:
                    stats1(n + 2 * TI)
                    if n % TI == TI - 1:
                        var1(n // TI + 2)
                if X2_LAG <= n < NT + X2_LAG:
                    mean2(n - X2_LAG)
                if n % TI == 1 and X2_LAG + TI < n <= NT + X2_LAG + 1:
                    var2((n - 1 - X2_LAG) // TI - 1)
                if n == 3:
                    block_scales(0)
                    common_scale(0, 0)
                if NT + 1 < n <= NT + OC + 1:
                    weights_lo(0, n - NT - 2, (n - 2) % 4)
                if n > H_LAG + 1:
                    h_max(n - H_LAG - 2)

            def quant_scale(scale, inv, tmp, rec, whole, factor):
                scalar2(col[tmp], col[whole], factor, 1.0 / QMAX)
                scalar2(col[scale], col[tmp], TINY, None, ALU.max, ALU.bypass)
                linked(nc.vector.reciprocal(col[rec], col[scale]))
                return nc.vector.tensor_scalar(col[inv], col[rec], factor, None, ALU.mult)

            dve.wait_ge(hcol_d, NT)
            nc.vector.tensor_reduce(col["hmx"], hcol, AX.X, ALU.max).then_inc(col_max, 1)
            dve.wait_ge(col_all, 2)
            quant_scale("xs", "xinv", "gt", "grc", "hall", 1.0).then_inc(xinv_d, 1)
            dve.wait_ge(x2_st, 16 * NG)
            for g in range(NG):
                dve.wait_ge(hq_d, g + 1)
                nc.vector.tensor_copy(XT[:, g, 0].rearrange("p k t -> p (k t)"), hq[:, g % 2]).then_inc(hhi_d, 1)
                dve.wait_ge(hhi_d, g + 1)
                nc.vector.tensor_tensor(XT[:, g, 1].rearrange("p k t -> p (k t)"), hq[:, g % 2],
                                        XT[:, g, 0].rearrange("p k t -> p (k t)"), ALU.subtract).then_inc(hlo_d, 1)
            scalar2(col["fg"], col["xs"], col["pw0"], 1.0)

            def gate_max(g, turned=None):
                for n in range(UPG):
                    dve.wait_ge(g_ev, g * UPG + n + 1)
                    nc.vector.tensor_reduce(gcol[:, bass.ds(g * UPG + n, 1)], gate_out[:, n % 2], AX.X, ALU.max,
                                            apply_absolute_value=True).then_inc(g_mx, 1)
                    if turned is not None:
                        for c in (2 * n, 2 * n + 1):
                            weights_lo(turned, c, 4 + c % 4)

            block_scales(1)
            common_scale(1, 2)
            gate_max(0)
            with nc.vector.Fori(1, 3) as g:
                gate_max(g)
            gate_max(3, 1)
            gate_max(4)
            block_scales(2)
            common_scale(2, 3)
            with nc.vector.Fori(5, 7) as g:
                gate_max(g)
            gate_max(7, 2)
            dve.wait_ge(g_mx, NU)
            nc.vector.tensor_reduce(col["gmx"], gcol, AX.X, ALU.max).then_inc(col_max, 1)
            dve.wait_ge(col_all, 5)
            quant_scale("gsc", "ginv", "gt", "grc", "gall", col["fg"]).then_inc(ginv_d, 1)
            scalar2(col["fu"], col["xs"], col["pw1"], 1.0)

            def up_max(n, s):
                dve.wait_ge(u_ev, n + 1)
                nc.vector.tensor_reduce(ucol[:, bass.ds(n, 1)], up_out[:, s], AX.X, ALU.max,
                                        apply_absolute_value=True).then_inc(u_mx, 1)

            def round_sig(v, j, late, base):
                dve.wait_ge(sig_d, base + v + 1)
                need(dve, a_mx if base == 0 else b_d, v)
                nc.vector.tensor_scalar(sigq, gate_in(j, late), 65536.0, 65535.0, ALU.mult, ALU.min).then_inc(r_d, 1)

            def act_max(v, j, late):
                dve.wait_ge(aq_d, v + 1)
                dve.wait_ge(r_d, v + 1)
                s = j % 2
                nc.vector.tensor_tensor_reduce(gate_in(j, late), aq[:, s], sigq, 1.0, scol[:, s:s + 1], ALU.mult, ALU.max,
                                               scol[:, s:s + 1]).then_inc(a_mx, 1)

            def act_int(v):
                dve.wait_ge(r_d, NU + v + 1)
                nc.vector.scalar_tensor_tensor(Q[:, v], Q[:, v], col["sinv"], sigq, ALU.mult, ALU.mult).then_inc(b_d, 1)

            def slot_a(n):
                v = 2 * n
                round_sig(v, v % 6, v >= 36, 0)
                up_max(n, n % 2)
                act_max(v, v % 6, v >= 36)
                round_sig(v + 1, (v + 1) % 6, v >= 36, 0)
                act_max(v + 1, (v + 1) % 6, v >= 36)

            def group_b(g):
                for n in range(UPG):
                    v = 12 * (g - 4) + 2 * n
                    round_sig(v, 2 * n % 6, True, NU)
                    up_max(g * UPG + n, n % 2)
                    act_int(v)
                    round_sig(v + 1, (2 * n + 1) % 6, True, NU)
                    act_int(v + 1)

            for n in range(NU // 2):
                slot_a(n)
            dve.wait_ge(a_mx, NU)
            nc.vector.tensor_reduce(col["smx"], scol, AX.X, ALU.max).then_inc(col_max, 1)
            scalar2(col["su"], col["gsc"], 1.0 / 65536.0, 1.0)
            dve.wait_ge(col_all, 6)
            linked(quant_scale("ssc", "sinv", "st", "src", "sall", col["su"]))
            group_b(4)
            with nc.vector.Fori(5, NG) as g:
                group_b(g)
            dve.wait_ge(u_mx, NU)
            nc.vector.tensor_reduce(col["umx"], ucol, AX.X, ALU.max).then_inc(col_max, 1)
            dve.wait_ge(col_all, 7)
            quant_scale("usc", "uinv", "ut", "urc", "uall", col["fu"]).then_inc(uinv_d, 1)
            scalar2(col["oo"], col["ssc"], col["usc"], 1.0)

            def o_max(t, k):
                n = 12 * t + k
                if k % 3 != 2:
                    dve.wait_ge(ag_d, 8 * t + 2 * (k // 3) + k % 3 + 1)
                else:
                    need(dve, o_mx, n - 3)
                    nc.vector.scalar_tensor_tensor(qb5[:, k % 4], Q[:, n], -1.0, Q[:, n], ALU.mult,
                                                   ALU.max).then_inc(agv_d, 1)
                    dve.wait_ge(agv_d, n // 3 + 1)
                dve.wait_ge(au_d, n + 1)
                nc.vector.tensor_tensor_reduce(ring5[:, k % 6], qa5[:, k % 4], qb5[:, k % 4], 1.0, ocol[:, k:k + 1], ALU.mult,
                                               ALU.max, ocol[:, k:k + 1]).then_inc(o_mx, 1)

            for t in range(4):
                for k in range(12):
                    o_max(t, k)
            dve.wait_ge(o_mx, NU)
            nc.vector.tensor_reduce(col["omx"], ocol, AX.X, ALU.max).then_inc(col_max, 1)
            dve.wait_ge(col_all, 8)
            linked(quant_scale("osc", "oinv", "ot", "orc", "oall", col["oo"]))
            scalar2(col["fin"], col["osc"], col["pw2"], 1.0)

            def o_int(t, k):
                n = 12 * t + k
                s, c = k // UPG, 2 * (k % UPG)
                hi = OT[:, s, 0, c:c + 2].rearrange("p c t -> p (c t)")
                lo = OT[:, s, 1, c:c + 2].rearrange("p c t -> p (c t)")
                if k % UPG == 0:
                    need(dve, dn_mm, 2 * (2 * t + s) - 2)
                dve.wait_ge(uq_d, n + 1)
                nc.vector.scalar_tensor_tensor(qb[:, k % 2], qa[:, k % 2], col["oinv"], Q[:, n], ALU.mult,
                                               ALU.mult).then_inc(oq_d, 1)
                dve.wait_ge(oq_d, n + 1)
                nc.vector.tensor_copy(hi, qb[:, k % 2]).then_inc(ohi_d, 1)
                dve.wait_ge(ohi_d, n + 1)
                nc.vector.tensor_tensor(lo, qb[:, k % 2], hi, ALU.subtract).then_inc(olo_d, 1)

            def finish(g, s):
                for r in range(2):
                    dve.wait_ge(dn_mm, 2 * g + r + 1)
                    dve.wait_ge(x2_ld[r], 16 * g + 16)
                    nc.vector.scalar_tensor_tensor(x2_in[:, r], ps[:, 4 * s + 2 * r:4 * s + 2 * r + 2].rearrange("p b w -> p (b w)"),
                                                   col["fin"], x2_in[:, r], ALU.mult, ALU.add).then_inc(fin_d, 1)

            for k in range(UPG):
                o_int(0, k)
            for k in range(UPG, 2 * UPG):
                o_int(0, k)
            finish(0, 0)
            with nc.vector.Fori(1, 4) as t:
                for k in range(UPG):
                    o_int(t, k)
                finish(2 * t - 1, 1)
                for k in range(UPG, 2 * UPG):
                    o_int(t, k)
                finish(2 * t, 0)
            finish(NG - 1, 1)


_INS = ['x', 'ctx_1024', 'L0_xattn_Wq', 'L0_xattn_Wkv', 'L0_ffn_w_gate', 'L0_ffn_w_up', 'L0_ffn_w_down']
_OUTS = [((B, S, D), 'float32')]


def kernel(**inputs):
    import numpy as _np
    import concourse.bacc as _bacc
    from concourse import mybir as _mybir
    from concourse.bass_utils import run_bass_kernel_spmd as _run

    nc = _bacc.Bacc("TRN2", target_bir_lowering=False, num_devices=1)
    arrays, args = {}, []
    for name in _INS:
        a = _np.ascontiguousarray(inputs[name])
        arrays[f"in_{name}_dram"] = a
        args.append(nc.dram_tensor(f"in_{name}_dram", a.shape, _mybir.dt.from_np(a.dtype), kind="ExternalInput").ap())
    for i, (shape, dtype) in enumerate(_OUTS):
        dt = _mybir.dt.from_np(_np.dtype(dtype))
        args.append(nc.dram_tensor(f"out_{i}_dram", shape, dt, kind="ExternalOutput").ap())
    build(nc, *args)
    r = _run(nc, [arrays], core_ids=[0])
    got = tuple(r.results[0][f"out_{i}_dram"] for i in range(len(_OUTS)))
    return got[0]
```

```python
from contextlib import ExitStack

import concourse.bass as bass
from concourse import mybir

P = 128
B, S, D = 2, 2048, 512
KV = 128
I = 1536
T = B * S
EPS = 1e-5
QMAX = 32767.0
TINY = 1e-12
BLK = 32
NG = T // 512
TI = 4
KC = D // P
OC = I // P
UPG = OC // 2
NU = NG * UPG
GPB = NG // B
UW = 1024
NBLK = OC * D // BLK
SCALE = float(D) ** -0.5
ROUND = 12582912.0
PV_LAG = TI + 3
X2_LAG = PV_LAG + 1
H_LAG = X2_LAG + TI + 3
W_SLOT = NG * TI + 4
WTOP = 2048.0

F32 = mybir.dt.float32
F16 = mybir.dt.float16
I16 = mybir.dt.int16
U16 = mybir.dt.uint16
I32 = mybir.dt.int32
ALU = mybir.AluOpType
ACT = mybir.ActivationFunctionType
AX = mybir.AxisListType
RMAX = bass.bass_isa.ReduceOp.max


def need(eng, sem, value):
    if isinstance(value, int) and value <= 0:
        return
    eng.wait_ge(sem, value)


def build(nc, x, ctx_in, wq_in, wkv_in, wg_in, wu_in, wd_in, out):
    x_v = x.rearrange("b (p j i) d -> b j p (i d)", p=P, j=GPB, i=TI)
    out_v = out.rearrange("b (p j i) d -> b j p (i d)", p=P, j=GPB, i=TI)
    gate_d = nc.dram_tensor("gate_park", [NU, P, UW], F32).ap()
    up_d = nc.dram_tensor("up_park", [NU, P, UW], F32).ap()
    x2_d = nc.dram_tensor("x2_park", [NG, P, TI * D], F32).ap()
    wd_d = nc.dram_tensor("wdown_park", [P, 12288], F16).ap()

    with ExitStack() as stack:
        def sem(name):
            return stack.enter_context(nc.semaphore(name))

        big = stack.enter_context(nc.sbuf_tensor("big", [P, 51200], F32))
        small = stack.enter_context(nc.sbuf_tensor("small", [P, 1840], F32))
        ps = stack.enter_context(nc.psum_tensor("ps", [P, 8, 512], F32))

        def part(start, words):
            return big[:, start:start + words]

        def cut(start, words):
            return small[:, start:start + words]

        X = part(0, 16384).rearrange("p (g i d) -> p g i d", g=NG, i=TI)
        XT = part(0, 16384).bitcast(F16).rearrange("p (g l k t) -> p g l k t", g=NG, l=2, k=KC)
        OT = part(0, 12288).bitcast(F16).rearrange("p (s l c t) -> p s l c t", s=2, l=2, c=OC)
        ring6 = part(12288, 4096).rearrange("p (s w) -> p s w", s=4)
        ring5 = part(6144, 6144).rearrange("p (s w) -> p s w", s=6)
        gate_s = part(4096, 2048).rearrange("p (s w) -> p s w", s=2)
        HT0 = 16384
        HT = part(HT0, 16384).rearrange("p (g k t) -> p g k t", g=NG, k=KC)
        ctx_sb = part(HT0 + 4096, 1024).rearrange("p (b d) -> p b d", b=B)
        ctxT = part(HT0 + 5120, 1024).rearrange("p (k b s) -> p k b s", k=KC, b=B)
        Vf = part(HT0 + 7168, 1024).rearrange("p (b d) -> p b d", b=B)
        KT = part(HT0 + 6144, 1024).rearrange("p (k s) -> p k s", k=KC)
        wkv = part(HT0 + 8192, 4096).rearrange("p (k n) -> p k n", k=KC)
        wqT = part(HT0 + 12288, 2048).rearrange("p (k n) -> p k n", k=KC)
        wq = part(HT0 + 14336, 2048).rearrange("p (k n) -> p k n", k=KC)
        gate_out = part(HT0, 2048).rearrange("p (s w) -> p s w", s=2)
        wd_prep = part(HT0 + 2048, 6144).bitcast(F16).rearrange("p (l c n) -> p l c n", l=2, c=OC)
        WG = part(32768, 6144).bitcast(F16).rearrange("p (l k o) -> p l k o", l=2, k=KC)
        WN = part(38912, 6144)
        U0 = 45056
        WU = part(U0, 6144).bitcast(F16).rearrange("p (l k o) -> p l k o", l=2, k=KC)
        WD = part(U0, 6144).bitcast(F16).rearrange("p (l c n) -> p l c n", l=2, c=OC)
        M = part(U0, 1024).rearrange("p (k b s) -> p k b s", k=KC, b=B)
        V = part(U0 + 1024, 1024).bitcast(F16).rearrange("p (l b d) -> p l b d", l=2, b=B)
        xTs = part(U0 + 2048, 1024).rearrange("p (s k t) -> p s k t", s=2, k=KC)
        Pe = part(U0 + 3072, 512).rearrange("p (i s) -> p i s", i=TI)
        PTs = part(HT0 + 14336, 1024).bitcast(F16).rearrange("p (s l i t) -> p s l i t", s=2, l=2, i=TI)
        h2 = part(U0 + 4096, 2048).rearrange("p (s d) -> p s d", s=4)
        hq = part(U0, 2048).bitcast(I16).rearrange("p (s w) -> p s w", s=2)
        Q = part(HT0, 24576).bitcast(I16).rearrange("p (u w) -> p u w", u=NU)
        up_out = part(40960, 2048).rearrange("p (s w) -> p s w", s=2)
        AHEAD = 4
        sweep_own = part(43008, 2048).rearrange("p (s w) -> p s w", s=2)
        sweep_early = part(36864, 4096).rearrange("p (s w) -> p s w", s=4)
        sweep_late = part(0, 4096).rearrange("p (s w) -> p s w", s=4)

        def gate_in(j, late):
            return sweep_own[:, j] if j < 2 else (sweep_late if late else sweep_early)[:, j - 2]

        def spare(v, k):
            return part((None, 0, 3072, 4096)[v // 12] + 512 * k, 512)

        def sig_int(v):
            return sigq if v % 2 == 0 or v < 12 else spare(v, 0).bitcast(U16)

        def magnitude(v):
            if v < 12:
                return aq[:, v % 2]
            return aq[:, v % 3] if v % 3 < 2 else spare(v, 1).bitcast(I16)

        qa5 = part(40960, 2048).bitcast(I16).rearrange("p (s w) -> p s w", s=4)
        qb5 = part(43008, 2048).bitcast(I16).rearrange("p (s w) -> p s w", s=4)
        qa = part(40960, 1024).bitcast(I16).rearrange("p (s w) -> p s w", s=2)
        qb = part(41984, 1024).bitcast(I16).rearrange("p (s w) -> p s w", s=2)
        x2_in = part(43008, 2048).rearrange("p (s w) -> p s w", s=2)

        bn = cut(0, 192).rearrange("p (n s) -> p n s", n=32)
        ve = cut(256, 32)
        rs1 = cut(288, 32)
        nmax = cut(320, 32)
        rsum = cut(352, 32)
        rinv = cut(384, 32)
        negm = cut(416, 32)
        xsum = cut(192, 32)
        ssq = cut(224, 32)
        rs2 = cut(448, 32)
        ve1 = cut(1504, 32)
        smax = cut(480, 32)
        mv = cut(1800, 16).rearrange("p (n s) -> p n s", n=8)
        wmean = cut(1816, 4)
        half = cut(512, 32)
        bmax = cut(544, 192)
        binv = cut(736, 192)
        bscl = cut(928, 192)
        ident = cut(1120, 128)
        squares = cut(1248, 256).bitcast(mybir.dt.bfloat16)
        aq = cut(0, 1024).bitcast(I16).rearrange("p (s w) -> p s w", s=2)
        sigq = cut(1024, 512).bitcast(U16)
        hcol = cut(1544, 32)
        gcol = cut(1544, 48)
        ucol = cut(1592, 48)
        scol = cut(1640, 2)
        ocol = cut(1688, 21)
        sc = cut(1736, 64)

        names = ("hmx hall gmx gall umx uall smx sall omx oall wmx0 wall0 wmx1 wall1 wmx2 wall2 "
                 "pw0 pw1 pw2 rpw xs xinv fg gt gsc grc ginv fu usc uinv ut urc st ssc sinv src su ot osc "
                 "oinv orc oo fin vmx vall vg vs vinv").split()
        col = {n: sc[:, k:k + 1] for k, n in enumerate(names)}

        x_ld = [sem(f"x_ld{g}") for g in range(NG)]
        ctx_ld, wq_ld, wk_ld, wv_ld = sem("ctx_ld"), sem("wq_ld"), sem("wk_ld"), sem("wv_ld")
        wg_ld = [sem("wg_ld0"), sem("wg_ld1")]
        wn_ld = {m: sem(f"wn_ld{m}") for m in (1, 2)}
        consts = sem("consts")
        pro_mm, pro_ev, pro_c = sem("pro_mm"), sem("pro_ev"), sem("pro_c")
        ve1_d, rs1_d = sem("ve1_d"), sem("rs1_d")
        xt_mm, xt_ev, sc_mm, nmax_d, exp_d = sem("xt_mm"), sem("xt_ev"), sem("sc_mm"), sem("nmax_d"), sem("exp_d")
        smax_d, rinv_d = sem("smax_d"), sem("rinv_d")
        pt_mm, pt_ev, av_mm, x2_d_s = sem("pt_mm"), sem("pt_ev"), sem("av_mm"), sem("x2_done")
        bn1_d, mv1_d, negm_d, ssq_d, ve2_d, rs2_d, h2_d = (sem(n) for n in
                                                           ("bn1_d", "mv1_d", "negm_d", "ssq_d", "ve2_d", "rs2_d", "h2_d"))
        v_d, plo_d = sem("v_d"), sem("plo_d")
        ht_mm, ht_ev, hcol_d, x2_st = sem("ht_mm"), sem("ht_ev"), sem("hcol_d"), sem("x2_st")
        w_blk, w_inv, w_rnd, w_deq = sem("w_blk"), sem("w_inv"), sem("w_rnd"), sem("w_deq")
        wt_mm, wt_hi, wt_lo, wd_st = sem("wt_mm"), sem("wt_hi"), sem("wt_lo"), sem("wd_st")
        wd_ld = [sem("wd_ld0"), sem("wd_ld1")]
        link = sem("link")
        col_max, col_all = sem("col_max"), sem("col_all")
        xinv_d, hq_d, hhi_d, hlo_d = sem("xinv_d"), sem("hq_d"), sem("hhi_d"), sem("hlo_d")
        g_mm, g_ev, g_mx = sem("g_mm"), sem("g_ev"), sem("g_mx")
        g_st = [sem("g_st0"), sem("g_st1")]
        u_mm, u_ev, u_mx = sem("u_mm"), sem("u_ev"), sem("u_mx")
        u_st = [sem("u_st0"), sem("u_st1")]
        g_ld = [sem(f"g_ld{j}") for j in range(6)]
        sinv_d, gs_d, si_d = sem("sinv_d"), sem("gs_d"), sem("si_d")
        ginv_d, q_d, aq_d, sig_d, r_d, a_mx, b_d = (sem(n) for n in
                                                  ("ginv_d", "q_d", "aq_d", "sig_d", "r_d", "a_mx", "b_d"))
        uinv_d, au_d, ag_d, pu_d, po_d, o_mx = (sem(n) for n in ("uinv_d", "au_d", "ag_d", "pu_d", "po_d", "o_mx"))
        r5_ld = [sem(f"r5_ld{s}") for s in range(6)]
        r6_ld = [sem(f"r6_ld{s}") for s in range(4)]
        uq_d, oq_d, ohi_d, olo_d = sem("uq_d"), sem("oq_d"), sem("ohi_d"), sem("olo_d")
        dn_mm, fin_d = sem("dn_mm"), sem("fin_d")
        x2_ld = [sem("x2_ld0"), sem("x2_ld1")]
        out_st = [sem("out_st0"), sem("out_st1")]

        block = stack.enter_context(nc.Block())

        def batch(g):
            return g // GPB

        @block.sync
        def _(sp):
            sp.dma_start(ctx_sb, ctx_in.rearrange("b s d -> s b d")).then_inc(ctx_ld, 16)
            sp.dma_start(wq, wq_in.rearrange("(k p) n -> p k n", p=P)).then_inc(wq_ld, 16)
            sp.dma_start(wkv[:, :, 0:D], wkv_in.rearrange("(k p) n -> p k n", p=P)[:, :, 0:D]).then_inc(wk_ld, 16)
            for g in range(NG):
                sp.dma_start(X[:, g].rearrange("p i d -> p (i d)"), x_v[g // GPB, g % GPB]).then_inc(x_ld[g], 16)
                if g == 0:
                    sp.dma_start(wkv[:, :, D:2 * D],
                                 wkv_in.rearrange("(k p) n -> p k n", p=P)[:, :, D:2 * D]).then_inc(wv_ld, 16)
                if g < 2:
                    c = slice(g * OC // 2, (g + 1) * OC // 2)
                    sp.dma_start(WN.rearrange("p (c d) -> p c d", c=OC)[:, c],
                                 wg_in.rearrange("(c p) d -> p c d", p=P)[:, c]).then_inc(wg_ld[g], 16)
            with nc.sync.Fori(0, NG) as g:
                sp.wait_ge(x2_d_s, TI * g + TI)
                sp.dma_start(x2_d[g], X[:, g].rearrange("p i d -> p (i d)")).then_inc(x2_st, 16)
            sp.wait_ge(wt_lo, OC)
            sp.dma_start(WN.rearrange("p (c d) -> p c d", c=OC),
                         wu_in.rearrange("(c p) d -> p c d", p=P)).then_inc(wn_ld[1], 16)

            def park_gate(g):
                for n in range(UPG):
                    sp.wait_ge(g_ev, g * UPG + n + 1)
                    sp.dma_start(gate_d[g * UPG + n], gate_out[:, n % 2]).then_inc(g_st[n % 2], 16)

            with nc.sync.Fori(0, 4) as g:
                park_gate(g)
            sp.wait_ge(wt_lo, 2 * OC)
            sp.dma_start(WN.rearrange("p (h n) -> p h n", h=KC),
                         wd_in.rearrange("(h p) n -> p h n", p=P)).then_inc(wn_ld[2], 16)
            with nc.sync.Fori(4, NG - 1) as g:
                park_gate(g)
            sp.wait_ge(wt_lo, 3 * OC)
            sp.dma_start(wd_d, wd_prep.rearrange("p l c n -> p (l c n)")).then_inc(wd_st, 16)

            def fetch_gate(v, j, late):
                need(sp, a_mx, v - 5)
                sp.dma_start(gate_in(j, late), gate_d[v]).then_inc(g_ld[j], 16)

            for s in range(2):
                sp.wait_ge(g_st[s], 16 * (NU - UPG) // 2)
            for v in range(2):
                fetch_gate(v, v, False)
            park_gate(NG - 1)

            def park_up(n, s):
                sp.wait_ge(u_ev, n + 1)
                sp.dma_start(up_d[n], up_out[:, s]).then_inc(u_st[s], 16)

            def group_a(g, last_late):
                for n in range(UPG):
                    park_up(g * UPG + n, n % 2)
                    for k in (2 * n + AHEAD, 2 * n + AHEAD + 1):
                        fetch_gate(12 * g + k, k % 6, last_late and k >= 12)

            sp.wait_ge(g_mm, NU)
            for v in range(2, AHEAD):
                fetch_gate(v, v, False)
            for s in range(2):
                sp.wait_ge(g_st[s], 16 * NU // 2)
            group_a(0, False)
            with nc.sync.Fori(1, 2) as g:
                group_a(g, False)
            group_a(2, True)
            for n in range(UPG):
                park_up(3 * UPG + n, n % 2)
                for k in (2 * n + AHEAD, 2 * n + AHEAD + 1):
                    if k < 12:
                        fetch_gate(36 + k, k % 6, True)
            with nc.sync.Fori(4, 6) as g:
                for n in range(UPG):
                    park_up(g * UPG + n, n % 2)
            sp.wait_ge(u_mm, 6 * UPG)
            for k in range(6):
                sp.dma_start(ring5[:, k], up_d[k]).then_inc(r5_ld[k], 16)
            with nc.sync.Fori(6, NG) as g:
                for n in range(UPG):
                    park_up(g * UPG + n, n % 2)
            for s in range(2):
                sp.wait_ge(u_st[s], 16 * NU // 2)
            with nc.sync.Fori(1, NU // 6) as t:
                for s in range(6):
                    sp.wait_ge(o_mx, 6 * t + s - 5)
                    sp.dma_start(ring5[:, s], up_d[6 * t + s]).then_inc(r5_ld[s], 16)
            sp.wait_ge(wd_st, 16)
            sp.wait_ge(u_mm, NU)
            wd_v = wd_d.rearrange("p (l c n) -> p l c n", l=2, c=OC)
            for r in range(2):
                for s in (2 * r, 2 * r + 1):
                    sp.dma_start(ring6[:, s], up_d[s]).then_inc(r6_ld[s], 16)
                c = slice(r * OC // 2, (r + 1) * OC // 2)
                sp.dma_start(WD[:, :, c], wd_v[:, :, c]).then_inc(wd_ld[r], 16)
            sp.wait_ge(x2_st, 16 * NG)
            sp.wait_ge(o_mx, NU)

            def fetch_x2(g, r):
                sp.dma_start(x2_in[:, r], x2_d[g, :, r * UW:(r + 1) * UW]).then_inc(x2_ld[r], 16)

            def store_out(b, j, g, r):
                sp.wait_ge(fin_d, 2 * g + r + 1)
                sp.dma_start(out_v[b, j, :, r * UW:(r + 1) * UW], x2_in[:, r]).then_inc(out_st[r], 16)

            def fetch_up(n, s):
                sp.wait_ge(uq_d, n - 3)
                sp.dma_start(ring6[:, s], up_d[n]).then_inc(r6_ld[s], 16)

            for r in range(2):
                fetch_x2(0, r)
            for n in range(4, 2 * UPG):
                fetch_up(n, n % 4)
            for s in range(2):
                for n in range(UPG):
                    fetch_up((s + 2) * UPG + n, (s * UPG + n) % 4)
                for r in range(2):
                    store_out(0, s, s, r)
                for r in range(2):
                    sp.wait_ge(out_st[r], 16 * (s + 1))
                    fetch_x2(s + 1, r)
            with nc.sync.Fori(1, 3) as t:
                for s in range(2):
                    g = 2 * t + s
                    for n in range(UPG):
                        fetch_up((g + 2) * UPG + n, (s * UPG + n) % 4)
                    for r in range(2):
                        store_out(batch(g), g % GPB, g, r)
                    for r in range(2):
                        sp.wait_ge(out_st[r], 16 * (g + 1))
                        fetch_x2(g + 1, r)
            for g in range(NG - 2, NG):
                for r in range(2):
                    store_out(g // GPB, g % GPB, g, r)
                if g < NG - 1:
                    for r in range(2):
                        sp.wait_ge(out_st[r], 16 * (g + 1))
                        fetch_x2(g + 1, r)
            for r in range(2):
                sp.wait_ge(out_st[r], 16 * NG)

        @block.gpsimd
        def _(pool):
            nc.gpsimd.memset(ident, 0.0).then_inc(consts, 1)
            nc.gpsimd.memset(half, -0.5).then_inc(consts, 1)
            pool.wait_ge(consts, 1)
            nc.gpsimd.affine_select(out=ident, in_=ident, compare_op=ALU.not_equal, fill=1.0, base=0,
                                    pattern=[[-1, P]], channel_multiplier=1).then_inc(consts, 1)
            pool.wait_ge(consts, 3)
            def rstd1(g):
                r = rs1[:, TI * g:TI * g + TI]
                pool.wait_ge(ve1_d, g + 1)
                nc.gpsimd.tensor_tensor(r, ve1[:, TI * g:TI * g + TI], half[:, TI * g:TI * g + TI],
                                        ALU.pow).then_inc(rs1_d, 1)
                pool.wait_ge(rs1_d, 2 * g + 1)
                nc.gpsimd.tensor_scalar(r, r, SCALE, 1.0, ALU.mult, ALU.mult).then_inc(rs1_d, 1)

            for g in range(2):
                rstd1(g)

            def all_max(k, src, dst):
                pool.wait_ge(col_max, k + 1)
                nc.gpsimd.partition_all_reduce(col[dst], col[src], P, RMAX).then_inc(col_all, 1)

            def quant_weights(at, blocks, base):
                w = WN[:, bass.ds(at * blocks * BLK, blocks * BLK)]
                wb = w.rearrange("p (n e) -> p n e", e=BLK)
                inv = binv[:, bass.ds(at * blocks, blocks)].unsqueeze(2).to_broadcast([P, blocks, BLK])
                scl = bscl[:, bass.ds(at * blocks, blocks)].unsqueeze(2).to_broadcast([P, blocks, BLK])
                nc.gpsimd.tensor_tensor(wb, wb, inv, ALU.mult).then_inc(w_inv, 1)
                pool.wait_ge(w_inv, base + at + 1)
                nc.gpsimd.tensor_scalar(w, w, ROUND, 1.0, ALU.add, ALU.mult).then_inc(w_rnd, 1)
                pool.wait_ge(w_rnd, 2 * base + 2 * at + 1)
                nc.gpsimd.tensor_scalar(w, w, -ROUND, 1.0, ALU.add, ALU.mult).then_inc(w_rnd, 1)
                pool.wait_ge(w_rnd, 2 * base + 2 * at + 2)
                nc.gpsimd.tensor_tensor(wb, wb, scl, ALU.mult).then_inc(w_deq, 1)

            def normalise(g):
                c = bass.ds(TI * g, TI)
                pool.wait_ge(ve2_d, g + 1)
                nc.gpsimd.tensor_tensor(rs2[:, c], ve[:, c], half[:, c], ALU.pow).then_inc(rs2_d, 1)
                pool.wait_ge(rs2_d, g + 1)
                for i in range(TI):
                    need(pool, ht_mm, TI * g + i - 3)
                    nc.gpsimd.tensor_scalar(h2[:, i], X[:, g, i], negm[:, bass.ds(TI * g + i, 1)],
                                            rs2[:, bass.ds(TI * g + i, 1)], ALU.add, ALU.mult).then_inc(h2_d, 1)

            all_max(0, "wmx0", "wall0")
            all_max(1, "vmx", "vall")
            pool.wait_ge(w_blk, 1)
            quant_weights(0, NBLK // 8, 0)
            rstd1(2)
            for at in (1, 2):
                quant_weights(at, NBLK // 8, 0)
            rstd1(3)
            for g in range(NG):
                normalise(g)
                if g < 4:
                    rstd1(g + 4)
                if g < 5:
                    quant_weights(g + 3, NBLK // 8, 0)
            all_max(2, "hmx", "hall")
            all_max(3, "wmx1", "wall1")
            pool.wait_ge(w_blk, 2)
            quant_weights(0, NBLK, 8)
            all_max(4, "wmx2", "wall2")
            pool.wait_ge(w_blk, 3)
            quant_weights(0, NBLK, 9)
            all_max(5, "gmx", "gall")
            pool.wait_ge(ginv_d, 1)
            pool.wait_ge(wd_st, 16)
            for s in range(2):
                pool.wait_ge(g_st[s], 16 * NU // 2)

            def gate_int(v):
                pool.wait_ge(g_ld[v % 6], 16 * (v // 6) + 16)
                if v >= 40:
                    pool.wait_ge(a_mx, 36)
                nc.gpsimd.tensor_scalar(Q[:, v], gate_in(v % 6, v >= 36), col["ginv"], 1.0,
                                        ALU.mult, ALU.mult).then_inc(q_d, 1)

            for v in range(NU):
                gate_int(v)
            all_max(6, "smx", "sall")
            pool.wait_ge(sinv_d, 1)
            pool.wait_ge(u_mm, 3 * UPG)
            for v in range(1, NU, 2):
                need(pool, b_d, v - 3)
                nc.gpsimd.tensor_scalar(gate_s[:, v // 2 % 2], Q[:, v], col["sinv"], 1.0,
                                        ALU.mult, ALU.mult).then_inc(gs_d, 1)
                pool.wait_ge(sig_d, NU + v + 1)
                nc.gpsimd.tensor_scalar(gate_in(v % 6, True).bitcast(I32), gate_in(v % 6, True), 65536.0, 1.0,
                                        ALU.mult, ALU.mult).then_inc(si_d, 1)
            all_max(7, "umx", "uall")
            pool.wait_ge(uinv_d, 1)
            for s in range(2):
                pool.wait_ge(u_st[s], 16 * NU // 2)
            for n in range(0, NU, 4):
                pool.wait_ge(r5_ld[n % 6], 16 * (n // 6) + 16)
                need(pool, o_mx, n - 3)
                nc.gpsimd.tensor_scalar(qa5[:, 0], ring5[:, n % 6], col["uinv"], 1.0, ALU.mult, ALU.mult).then_inc(pu_d, 1)
            all_max(8, "omx", "oall")

        @block.tensor
        def _(pe):
            def turn(dst, src):
                return nc.tensor.transpose(dst, src, ident)

            pe.wait_ge(consts, 3)
            pe.wait_ge(ctx_ld, 16)
            for b in range(B):
                for k in range(KC):
                    mm = turn(ps[:, b, k * P:(k + 1) * P], ctx_sb[:, b, k * P:(k + 1) * P])
                mm.then_inc(pro_mm, 1)
            pe.wait_ge(wq_ld, 16)
            for k in range(KC):
                for m in range(KC):
                    mm = turn(ps[:, 4 + k, m * P:(m + 1) * P], wq[:, k, m * P:(m + 1) * P])
                mm.then_inc(pro_mm, 1)
            pe.wait_ge(wk_ld, 16)
            pe.wait_ge(pro_ev, 2)
            for m in range(KC):
                for k in range(KC):
                    mm = nc.tensor.matmul(ps[:, 2 + m // 2, (m % 2) * 256:(m % 2) * 256 + 256],
                                          wkv[:, k, m * P:(m + 1) * P],
                                          ctxT[:, k].rearrange("p b s -> p (b s)"), start=(k == 0), stop=(k == KC - 1))
                if m % 2:
                    mm.then_inc(pro_mm, 1)

            def value(b):
                for k in range(KC):
                    mm = nc.tensor.matmul(ps[:, 4 + b], ctxT[:, k, b], wkv[:, k, D:2 * D],
                                          start=(k == 0), stop=(k == KC - 1))
                mm.then_inc(pro_mm, 1)

            pe.wait_ge(wv_ld, 16)
            pe.wait_ge(pro_ev, 6)
            value(0)
            pe.wait_ge(pro_ev, 8)
            pe.wait_ge(pro_c, 1)
            for h in range(KC):
                for m in range(KC):
                    mm = nc.tensor.matmul(ps[:, 6 + h // 2, (h % 2) * 256:(h % 2) * 256 + 256],
                                          wqT[:, m, h * P:(h + 1) * P], KT[:, m],
                                          start=(m == 0), stop=(m == KC - 1))
                if h % 2:
                    mm.then_inc(pro_mm, 1)
            value(1)

            NT = NG * TI

            def turn_x(n):
                if n % TI == 0:
                    pe.wait_ge(x_ld[n // TI], 16)
                need(pe, xt_ev, n - 1)
                for k in range(KC):
                    mm = turn(ps[:, n % 2, k * P:(k + 1) * P], X[:, n // TI, n % TI, k * P:(k + 1) * P])
                mm.then_inc(xt_mm, 1)

            def scores(n):
                g, i = n // TI, n % TI
                if i == 0:
                    need(pe, exp_d, TI * (g - 1))
                pe.wait_ge(xt_ev, n + 1)
                for k in range(KC):
                    mm = nc.tensor.matmul(ps[:, 2 + g % 2, i * P:(i + 1) * P], xTs[:, n % 2, k], M[:, k, batch(g)],
                                          start=(k == 0), stop=(k == KC - 1))
                mm.then_inc(sc_mm, 1)

            def turn_p(g):
                need(pe, plo_d, g)
                for i in range(TI):
                    pe.wait_ge(exp_d, TI * g + i + 1)
                    mm = turn(ps[:, 4, i * P:(i + 1) * P], Pe[:, i])
                mm.then_inc(pt_mm, 1)

            def attend(n):
                if n == 0:
                    pe.wait_ge(v_d, 2)
                pe.wait_ge(plo_d, n // TI + 1)
                need(pe, x2_d_s, n - 1)
                for a, b in ((0, 0), (0, 1), (1, 0)):
                    mm = nc.tensor.matmul(ps[:, 5 + n % 2], PTs[:, n // TI % 2, a, n % TI], V[:, b, batch(n // TI)],
                                          start=(a + b == 0), stop=(a == 1))
                mm.then_inc(av_mm, 1)

            def turn_h(n):
                need(pe, ht_ev, n)
                pe.wait_ge(h2_d, n + 1)
                for k in range(KC):
                    mm = turn(ps[:, 7, k * P:(k + 1) * P], h2[:, n % 4, k * P:(k + 1) * P])
                mm.then_inc(ht_mm, 1)

            def turn_weights(m, c, bank, gap):
                if c == 0:
                    pe.wait_ge(w_deq, 8 + m)
                if c >= gap:
                    pe.wait_ge(wt_lo, m * OC + c - gap + 1)
                for k in range(KC):
                    at = k * I + c * P if m == 2 else c * D + k * P
                    mm = turn(ps[:, bank, k * P:(k + 1) * P], WN[:, at:at + P])
                mm.then_inc(wt_mm, 1)

            turn_x(0)
            pe.wait_ge(pro_ev, 12)
            for n in range(NT + H_LAG + 1):
                if n + 1 < NT:
                    turn_x(n + 1)
                if n % TI == 2 and TI <= n < NT + TI:
                    turn_p(n // TI - 1)
                if n < NT:
                    scores(n)
                if PV_LAG <= n < NT + PV_LAG:
                    attend(n - PV_LAG)
                if W_SLOT <= n < W_SLOT + OC:
                    if n == W_SLOT:
                        pe.wait_ge(xt_ev, NT)
                        pe.wait_ge(exp_d, NT)
                    turn_weights(0, n - W_SLOT, n % 4, 4)
                if H_LAG <= n < NT + H_LAG:
                    turn_h(n - H_LAG)

            def unit(w, g, n, done):
                for j in range(2):
                    o = (2 * n + j) * P
                    for k in range(KC):
                        if done is g_mm and isinstance(g, int) and g + n + j == 0:
                            pe.wait_ge(hlo_d, k + 1)
                        for a, b in ((0, 0), (1, 0), (0, 1)):
                            mm = nc.tensor.matmul(ps[:, 2 * (n % 2) + j], w[:, a, k, o:o + P], XT[:, g, b, k],
                                                  start=(k == 0 and a + b == 0), stop=(k == KC - 1 and b == 1))
                mm.then_inc(done, 1)

            def product(w, g, mm_sem, ev_sem, turned=None):
                for n in range(UPG):
                    need(pe, ev_sem, g * UPG + n - 1)
                    unit(w, g, n, mm_sem)
                    if turned is not None:
                        for c in (2 * n, 2 * n + 1):
                            turn_weights(turned, c, 4 + c % 4, 4)

            def gate(g, turned=None):
                if not (isinstance(g, int) and g == 0):
                    pe.wait_ge(hlo_d, g + KC)
                product(WG, g, g_mm, g_ev, turned)

            pe.wait_ge(wt_lo, OC)
            gate(0)
            with nc.tensor.Fori(1, 3) as g:
                gate(g)
            gate(3, 1)
            with nc.tensor.Fori(4, 6) as g:
                gate(g)
            gate(6, 2)
            gate(7)
            pe.wait_ge(wt_lo, 2 * OC)
            pe.wait_ge(g_ev, NU)
            product(WU, 0, u_mm, u_ev)
            with nc.tensor.Fori(1, NG) as g:
                product(WU, g, u_mm, u_ev)

            def down(g, s):
                need(pe, fin_d, 2 * g - 2)
                for n in range(UPG):
                    if s == 0 and isinstance(g, int) and 2 * n == OC // 2:
                        pe.wait_ge(wd_ld[1], 16)
                    pe.wait_ge(olo_d, g * UPG + n + 1)
                    for i in range(TI):
                        for c in (2 * n, 2 * n + 1):
                            for a, b in ((0, 0), (0, 1), (1, 0)):
                                mm = nc.tensor.matmul(ps[:, 4 * s + i], OT[:, s, a, c, i * P:(i + 1) * P], WD[:, b, c],
                                                      start=(c == 0 and a + b == 0), stop=(c == OC - 1 and a == 1))
                        if n == UPG - 1 and i % 2:
                            mm.then_inc(dn_mm, 1)

            pe.wait_ge(wd_ld[0], 16)
            pe.wait_ge(u_ev, NU)
            down(0, 0)
            down(1, 1)
            with nc.tensor.Fori(1, NG // 2) as t:
                for s in range(2):
                    down(2 * t + s, s)

        @block.scalar
        def _(act):
            def copy(dst, src):
                return nc.scalar.activation(dst, src, ACT.Copy)

            for b in range(B):
                act.wait_ge(pro_mm, b + 1)
                copy(ctxT[:, :, b], ps[:, b].rearrange("p (k s) -> p k s", k=KC)).then_inc(pro_ev, 1)
            for k in range(KC):
                act.wait_ge(pro_mm, k + 3)
                copy(wqT[:, :, k * P:(k + 1) * P], ps[:, 4 + k].rearrange("p (m s) -> p m s", m=KC)).then_inc(pro_ev, 1)
            for m in range(2):
                act.wait_ge(pro_mm, m + 7)
                copy(KT[:, 2 * m:2 * m + 2], ps[:, 2 + m].rearrange("p (k s) -> p k s", k=2)).then_inc(pro_ev, 1)
            act.wait_ge(pro_mm, 9)
            copy(Vf[:, 0], ps[:, 4]).then_inc(pro_ev, 1)
            for m in range(2):
                act.wait_ge(pro_mm, m + 10)
                copy(M[:, 2 * m:2 * m + 2].rearrange("p k b s -> p k (b s)"),
                     ps[:, 6 + m].rearrange("p (k s) -> p k s", k=2)).then_inc(pro_ev, 1)
            act.wait_ge(pro_mm, 12)
            copy(Vf[:, 1], ps[:, 5]).then_inc(pro_ev, 1)

            NT = NG * TI

            def take_xT(n):
                act.wait_ge(xt_mm, n + 1)
                need(act, sc_mm, n - 1)
                copy(xTs[:, n % 2], ps[:, n % 2].rearrange("p (k t) -> p k t", k=KC)).then_inc(xt_ev, 1)

            def exps(n):
                g, i = n // TI, n % TI
                act.wait_ge(nmax_d, g + 1)
                need(act, pt_mm, g)
                nc.scalar.activation(Pe[:, i], ps[:, 2 + g % 2, i * P:(i + 1) * P], ACT.Exp, bias=nmax[:, n:n + 1],
                                     scale=rs1[:, n:n + 1], accum_out=rsum[:, n:n + 1]).then_inc(exp_d, 1)

            def take_pT(g):
                act.wait_ge(pt_mm, g + 1)
                need(act, av_mm, TI * (g - 1))
                copy(PTs[:, g % 2, 0], ps[:, 4].rearrange("p (i t) -> p i t", i=TI)).then_inc(pt_ev, 1)

            def spread(n):
                act.wait_ge(negm_d, n + 1)
                need(act, ssq_d, n)
                nc.scalar.activation(squares, X[:, n // TI, n % TI], ACT.Square, bias=negm[:, n:n + 1],
                                     accum_out=ssq[:, n:n + 1]).then_inc(ssq_d, 1)

            def take_hT(n):
                act.wait_ge(ht_mm, n + 1)
                t = (n % TI) * P
                copy(HT[:, n // TI, :, t:t + P], ps[:, 7].rearrange("p (k t) -> p k t", k=KC)).then_inc(ht_ev, 1)

            def weights_hi(m, c, bank):
                act.wait_ge(wt_mm, m * OC + c + 1)
                src = ps[:, bank]
                if m == 2:
                    dst = wd_prep[:, 0, c]
                else:
                    dst = (WG, WU)[m][:, 0, :, c * P:(c + 1) * P]
                    src = src.rearrange("p (k o) -> p k o", k=KC)
                copy(dst, src).then_inc(wt_hi, 1)

            take_xT(0)
            for n in range(NT + H_LAG + 2):
                if n + 1 < NT:
                    take_xT(n + 1)
                if H_LAG < n <= NT + H_LAG:
                    take_hT(n - H_LAG - 1)
                if n % TI == 1 and TI <= n < NT + TI:
                    for i in (2, 3):
                        exps(n - 1 - TI + i)
                if X2_LAG < n <= NT + X2_LAG:
                    spread(n - X2_LAG - 1)
                if W_SLOT < n <= W_SLOT + OC:
                    weights_hi(0, n - W_SLOT - 1, (n - 1) % 4)
                if n % TI == 0 and TI <= n < NT + TI:
                    for i in (0, 1):
                        exps(n - TI + i)
                if n % TI == 2 and TI <= n < NT + TI:
                    take_pT(n // TI - 1)

            act.wait_ge(xinv_d, 1)
            for k in range(KC):
                nc.scalar.activation(hq[:, 0, k * 512:(k + 1) * 512], HT[:, 0, k], ACT.Copy,
                                     scale=col["xinv"]).then_inc(hq_d, 1)

            def h_int(g):
                need(act, hlo_d, g + KC - 2 if g > 1 else 0)
                nc.scalar.activation(hq[:, g % 2], HT[:, g].rearrange("p k t -> p (k t)"), ACT.Copy,
                                     scale=col["xinv"]).then_inc(hq_d, 1)

            h_int(1)

            def take_gate(g, turned=None):
                for n in range(UPG):
                    act.wait_ge(g_mm, g * UPG + n + 1)
                    need(act, g_mx, g * UPG + n - 1)
                    if not (isinstance(g, int) and g == 0 and n < 2):
                        act.wait_ge(g_st[n % 2], 16 * (g * (UPG // 2) + n // 2))
                    copy(gate_out[:, n % 2], ps[:, 2 * (n % 2):2 * (n % 2) + 2].rearrange("p b w -> p (b w)")).then_inc(g_ev, 1)
                    if isinstance(g, int) and g == 0 and n + 2 < NG:
                        h_int(n + 2)
                    if turned is not None:
                        for c in (2 * n, 2 * n + 1):
                            weights_hi(turned, c, 4 + c % 4)

            take_gate(0)
            with nc.scalar.Fori(1, 3) as g:
                take_gate(g)
            take_gate(3, 1)
            with nc.scalar.Fori(4, 6) as g:
                take_gate(g)
            take_gate(6, 2)
            take_gate(7)

            def take_up(n, s, first):
                act.wait_ge(u_mm, n + 1)
                if not first:
                    act.wait_ge(u_mx, n - 1)
                    act.wait_ge(u_st[s], 8 * (n - s))
                copy(up_out[:, s], ps[:, 2 * s:2 * s + 2].rearrange("p b w -> p (b w)")).then_inc(u_ev, 1)

            def sweep_a(v):
                act.wait_ge(g_ld[v % 6], 16 * (v // 6) + 16)
                need(act, a_mx, v - 1 if v < 14 else v - 2)
                nc.scalar.activation(magnitude(v), gate_in(v % 6, v >= 36), ACT.Abs, scale=col["ginv"]).then_inc(aq_d, 1)

            def sigmoid(v):
                act.wait_ge(q_d, v + 1)
                act.wait_ge(aq_d, v + 1)
                nc.scalar.activation(gate_in(v % 6, v >= 36), Q[:, v], ACT.Sigmoid, scale=col["gsc"]).then_inc(sig_d, 1)

            def sweep_b(g, k):
                v = 12 * (g - 4) + k
                if isinstance(g, int) and g == 4 and k < 6:
                    act.wait_ge(a_mx, NU - 5 + k)
                else:
                    act.wait_ge(b_d, v - 5)
                nc.scalar.activation(gate_in(k % 6, True), Q[:, v], ACT.Sigmoid, scale=col["gsc"]).then_inc(sig_d, 1)

            def group_b(g):
                for n in range(UPG):
                    sweep_b(g, 2 * n)
                    sweep_b(g, 2 * n + 1)
                    if not (isinstance(g, int) and g == 4 and n == 0):
                        take_up(g * UPG + n, n % 2, False)

            act.wait_ge(wt_lo, 3 * OC)
            take_up(0, 0, True)
            act.wait_ge(ginv_d, 1)
            sweep_a(0)
            for n in range(NU // 2):
                sigmoid(2 * n)
                sweep_a(2 * n + 1)
                take_up(n + 1, (n + 1) % 2, n == 0)
                sigmoid(2 * n + 1)
                if n < NU // 2 - 1:
                    sweep_a(2 * n + 2)
            group_b(4)
            with nc.scalar.Fori(5, NG) as g:
                group_b(g)

            def act_magnitude(n, s):
                nc.scalar.activation(qb5[:, s], Q[:, n], ACT.Abs).then_inc(ag_d, 1)

            act.wait_ge(b_d, NU)
            for n in range(1, 4):
                act_magnitude(n, n)
            act.wait_ge(uinv_d, 1)
            for s in range(2):
                act.wait_ge(u_st[s], 16 * NU // 2)

            def magnitudes(t, k):
                s = k % 6
                n = 12 * t + k
                act.wait_ge(r5_ld[s], 16 * (2 * t + k // 6) + 16)
                need(act, o_mx, n - 3)
                nc.scalar.activation(qa5[:, k % 4], ring5[:, s], ACT.Abs, scale=col["uinv"]).then_inc(au_d, 1)
                if not (isinstance(t, int) and k < 4):
                    act_magnitude(n, k % 4)

            for k in range(12):
                if k % 4:
                    magnitudes(0, k)
            with nc.scalar.Fori(1, 4) as t:
                for k in range(12):
                    if k % 4:
                        magnitudes(t, k)

            def up_int(t, k):
                s = k % 4
                n = 12 * t + k
                act.wait_ge(r6_ld[s], 16 * (3 * t + k // 4) + 16)
                need(act, oq_d, n - 1)
                nc.scalar.activation(qa[:, k % 2], ring6[:, s], ACT.Copy, scale=col["uinv"]).then_inc(uq_d, 1)

            act.wait_ge(o_mx, NU)
            for k in range(12):
                up_int(0, k)
            with nc.scalar.Fori(1, 4) as t:
                for k in range(12):
                    up_int(t, k)

        @block.vector
        def _(dve):
            count = [0]

            def linked(ins):
                count[0] += 1
                ins.then_inc(link, 1)
                dve.wait_ge(link, count[0])

            def scalar2(dst, src, s1, s2, op0=ALU.mult, op1=ALU.mult):
                linked(nc.vector.tensor_scalar(dst, src, s1, s2, op0, op1))

            linked(nc.vector.memset(scol, 0.0))
            linked(nc.vector.memset(ocol, 0.0))
            def block_max(at, parts, ready):
                n = NBLK // parts
                dve.wait_ge(ready, 16)
                return nc.vector.tensor_reduce(bmax[:, at * n:(at + 1) * n],
                                               WN[:, at * n * BLK:(at + 1) * n * BLK].rearrange("p (n e) -> p n e", e=BLK),
                                               AX.X, ALU.max, apply_absolute_value=True)

            def block_scales(m):
                scalar2(bscl, bmax, 1.0 / 7.0, TINY, ALU.mult, ALU.max)
                linked(nc.vector.reciprocal(binv, bscl))
                nc.vector.tensor_reduce(col[f"wmx{m}"], bscl, AX.X, ALU.max).then_inc(col_max, 1)

            def power_of_two(power, inv, whole):
                linked(nc.vector.tensor_scalar(col[inv].bitcast(I32), col[whole].bitcast(I32), 0x7F800000, None,
                                               ALU.bitwise_and))
                scalar2(col[power], col[inv], 1.0 / WTOP, 1.0)
                linked(nc.vector.reciprocal(col[inv], col[power]))

            def common_scale(m, k):
                dve.wait_ge(col_all, k + 1)
                power_of_two(f"pw{m}", "rpw", f"wall{m}")
                nc.vector.tensor_scalar(bscl, bscl, col["rpw"], None, ALU.mult).then_inc(w_blk, 1)

            NT = NG * TI

            def stats1(n):
                if n % TI == 0:
                    dve.wait_ge(x_ld[n // TI], 16)
                nc.vector.bn_stats(bn[:, n], X[:, n // TI, n % TI]).then_inc(bn1_d, 1)

            def var1(g):
                dve.wait_ge(bn1_d, TI * g + TI)
                for i in range(TI):
                    nc.vector.bn_aggr(mv[:, i], bn[:, TI * g + i]).then_inc(mv1_d, 1)
                dve.wait_ge(mv1_d, TI * g + TI)
                nc.vector.tensor_scalar(ve1[:, TI * g:TI * g + TI], mv[:, 0:TI, 1], EPS, None,
                                        ALU.add).then_inc(ve1_d, 1)

            def score_max(g):
                c = slice(TI * g, TI * g + TI)
                dve.wait_ge(sc_mm, TI * g + TI)
                nc.vector.tensor_reduce(smax[:, c], ps[:, 2 + g % 2].rearrange("p (i s) -> p i s", i=TI), AX.X,
                                        ALU.max).then_inc(smax_d, 1)
                dve.wait_ge(smax_d, g + 1)
                dve.wait_ge(rs1_d, 2 * g + 2)
                nc.vector.scalar_tensor_tensor(nmax[:, c], smax[:, c], -1.0, rs1[:, c], ALU.mult,
                                               ALU.mult).then_inc(nmax_d, 1)

            def residual(n):
                g, i = n // TI, n % TI
                if i == 0:
                    dve.wait_ge(exp_d, TI * g + TI)
                    r = rinv[:, n:n + TI]
                    nc.vector.reciprocal(r, rsum[:, n:n + TI]).then_inc(rinv_d, 1)
                    dve.wait_ge(rinv_d, 2 * g + 1)
                    nc.vector.tensor_scalar(r, r, col["vs"], None, ALU.mult).then_inc(rinv_d, 1)
                    dve.wait_ge(rinv_d, 2 * g + 2)
                dve.wait_ge(av_mm, n + 1)
                nc.vector.scalar_tensor_tensor(X[:, g, i], ps[:, 5 + n % 2], rinv[:, n:n + 1], X[:, g, i],
                                               ALU.mult, ALU.add, accum_out=xsum[:, n:n + 1]).then_inc(x2_d_s, 1)

            def p_lo(g):
                dve.wait_ge(pt_ev, g + 1)
                nc.vector.tensor_tensor(PTs[:, g % 2, 1], ps[:, 4].rearrange("p (i t) -> p i t", i=TI), PTs[:, g % 2, 0],
                                        ALU.subtract).then_inc(plo_d, 1)

            def mean2(n):
                dve.wait_ge(x2_d_s, n + 1)
                nc.vector.tensor_scalar(negm[:, n:n + 1], xsum[:, n:n + 1], -1.0 / D, None, ALU.mult).then_inc(negm_d, 1)

            def var2(g):
                c = slice(TI * g, TI * g + TI)
                dve.wait_ge(ssq_d, TI * g + TI)
                nc.vector.tensor_scalar(ve[:, c], ssq[:, c], 1.0 / D, EPS, ALU.mult, ALU.add).then_inc(ve2_d, 1)

            def h_max(n):
                dve.wait_ge(ht_ev, n + 1)
                t = (n % TI) * P
                nc.vector.tensor_reduce(hcol[:, n:n + 1], HT[:, n // TI, :, t:t + P], AX.XY, ALU.max,
                                        apply_absolute_value=True).then_inc(hcol_d, 1)

            def weights_lo(m, c, bank):
                dve.wait_ge(wt_hi, m * OC + c + 1)
                src = ps[:, bank]
                if m == 2:
                    hi, lo = wd_prep[:, 0, c], wd_prep[:, 1, c]
                else:
                    hi, lo = ((WG, WU)[m][:, l, :, c * P:(c + 1) * P] for l in range(2))
                    src = src.rearrange("p (k o) -> p k o", k=KC)
                nc.vector.tensor_tensor(lo, src, hi, ALU.subtract).then_inc(wt_lo, 1)

            dve.wait_ge(pro_ev, 6)
            linked(nc.vector.tensor_reduce(wmean, wqT, AX.X, ALU.add))
            scalar2(wmean, wmean, -1.0 / D, 1.0)
            for m in range(KC):
                last = nc.vector.tensor_scalar(wqT[:, m], wqT[:, m], wmean[:, m:m + 1], None, ALU.add)
            last.then_inc(pro_c, 1)
            for g in range(2):
                for i in range(TI):
                    stats1(TI * g + i)
                var1(g)
                linked(block_max(g, 2, wg_ld[g]))
            for n in range(NT + H_LAG + 2):
                if n % TI == 0 and TI <= n < NT + TI:
                    score_max(n // TI - 1)
                if X2_LAG <= n < NT + X2_LAG:
                    residual(n - X2_LAG)
                if n % TI == 3 and TI <= n < NT + TI:
                    p_lo(n // TI - 1)
                if n + 2 * TI < NT:
                    stats1(n + 2 * TI)
                    if n % TI == TI - 1:
                        var1(n // TI + 2)
                if X2_LAG <= n < NT + X2_LAG:
                    mean2(n - X2_LAG)
                if n % TI == 1 and X2_LAG + TI < n <= NT + X2_LAG + 1:
                    var2((n - 1 - X2_LAG) // TI - 1)
                if n == 0:
                    block_scales(0)
                if n == 1:
                    common_scale(0, 0)
                if n == 0:
                    dve.wait_ge(pro_ev, 12)
                    nc.vector.tensor_reduce(col["vmx"], Vf, AX.XY, ALU.max, apply_absolute_value=True).then_inc(col_max, 1)
                if n == 2:
                    dve.wait_ge(col_all, 2)
                    scalar2(col["vg"], col["vall"], TINY, None, ALU.max, ALU.bypass)
                    power_of_two("vs", "vinv", "vg")
                    nc.vector.tensor_scalar(V[:, 0], Vf, col["vinv"], None, ALU.mult).then_inc(v_d, 1)
                if n == 4:
                    dve.wait_ge(v_d, 1)
                    nc.vector.scalar_tensor_tensor(V[:, 1], Vf, col["vinv"], V[:, 0], ALU.mult, ALU.subtract).then_inc(v_d, 1)
                if H_LAG + 1 < n <= NT + H_LAG + 1:
                    h_max(n - H_LAG - 2)
                if W_SLOT + 1 < n <= H_LAG + NT:
                    weights_lo(0, n - W_SLOT - 2, (n - 2) % 4)

            def quant_scale(scale, inv, tmp, rec, whole, factor):
                scalar2(col[tmp], col[whole], factor, 1.0 / QMAX)
                scalar2(col[scale], col[tmp], TINY, None, ALU.max, ALU.bypass)
                linked(nc.vector.reciprocal(col[rec], col[scale]))
                return nc.vector.tensor_scalar(col[inv], col[rec], factor, None, ALU.mult)

            dve.wait_ge(hcol_d, NT)
            nc.vector.tensor_reduce(col["hmx"], hcol, AX.X, ALU.max).then_inc(col_max, 1)
            for c in range(H_LAG + NT - 1 - W_SLOT, OC):
                weights_lo(0, c, (W_SLOT + c) % 4)
            dve.wait_ge(col_all, 3)
            quant_scale("xs", "xinv", "gt", "grc", "hall", 1.0).then_inc(xinv_d, 1)
            dve.wait_ge(x2_st, 16 * NG)
            for k in range(KC):
                src, hi, lo = hq[:, 0, k * 512:(k + 1) * 512], XT[:, 0, 0, k], XT[:, 0, 1, k]
                dve.wait_ge(hq_d, k + 1)
                nc.vector.tensor_copy(hi, src).then_inc(hhi_d, 1)
                dve.wait_ge(hhi_d, k + 1)
                nc.vector.tensor_tensor(lo, src, hi, ALU.subtract).then_inc(hlo_d, 1)

            def split_h(g):
                hi, lo = (XT[:, g, l].rearrange("p k t -> p (k t)") for l in range(2))
                dve.wait_ge(hq_d, g + KC)
                nc.vector.tensor_copy(hi, hq[:, g % 2]).then_inc(hhi_d, 1)
                dve.wait_ge(hhi_d, g + KC)
                nc.vector.tensor_tensor(lo, hq[:, g % 2], hi, ALU.subtract).then_inc(hlo_d, 1)

            split_h(1)
            scalar2(col["fg"], col["xs"], col["pw0"], 1.0)

            def gate_max(g, turned=None, units=range(UPG)):
                for n in units:
                    dve.wait_ge(g_ev, g * UPG + n + 1)
                    nc.vector.tensor_reduce(gcol[:, bass.ds(g * UPG + n, 1)], gate_out[:, n % 2], AX.X, ALU.max,
                                            apply_absolute_value=True).then_inc(g_mx, 1)
                    if isinstance(g, int) and g == 0 and n + 2 < NG:
                        split_h(n + 2)
                    if turned is not None:
                        for c in (2 * n, 2 * n + 1):
                            weights_lo(turned, c, 4 + c % 4)

            gate_max(0)
            linked(block_max(0, 1, wn_ld[1]))
            block_scales(1)
            common_scale(1, 3)
            with nc.vector.Fori(1, 3) as g:
                gate_max(g)
            gate_max(3, 1)
            gate_max(4, units=range(2))
            linked(block_max(0, 1, wn_ld[2]))
            block_scales(2)
            common_scale(2, 4)
            gate_max(4, units=range(2, UPG))
            gate_max(5)
            gate_max(6, 2)
            gate_max(7)
            dve.wait_ge(g_mx, NU)
            nc.vector.tensor_reduce(col["gmx"], gcol, AX.X, ALU.max).then_inc(col_max, 1)
            dve.wait_ge(col_all, 6)
            quant_scale("gsc", "ginv", "gt", "grc", "gall", col["fg"]).then_inc(ginv_d, 1)
            scalar2(col["fu"], col["xs"], col["pw1"], 1.0)

            def up_max(n, s):
                dve.wait_ge(u_ev, n + 1)
                nc.vector.tensor_reduce(ucol[:, bass.ds(n, 1)], up_out[:, s], AX.X, ALU.max,
                                        apply_absolute_value=True).then_inc(u_mx, 1)

            def round_sig(dst, src):
                nc.vector.tensor_scalar(dst, src, 65536.0, 65535.0, ALU.mult, ALU.min).then_inc(r_d, 1)

            def round_a(v):
                dve.wait_ge(sig_d, v + 1)
                need(dve, a_mx, v - 1 if v > 12 else v)
                round_sig(sig_int(v), gate_in(v % 6, v >= 36))

            def act_max(v):
                dve.wait_ge(aq_d, v + 1)
                dve.wait_ge(r_d, v + 1)
                s = v % 2
                nc.vector.tensor_tensor_reduce(gate_in(v % 6, v >= 36), magnitude(v), sig_int(v), 1.0, scol[:, s:s + 1],
                                               ALU.mult, ALU.max, scol[:, s:s + 1]).then_inc(a_mx, 1)

            def act_int(m):
                v = 2 * m
                dve.wait_ge(r_d, NU + m + 1)
                nc.vector.scalar_tensor_tensor(Q[:, v], Q[:, v], col["sinv"], sigq, ALU.mult, ALU.mult).then_inc(b_d, 1)

            def act_int_odd(m, j, s):
                v = 2 * m + 1
                dve.wait_ge(gs_d, m + 1)
                dve.wait_ge(si_d, m + 1)
                nc.vector.scalar_tensor_tensor(Q[:, v], gate_in(j, True).bitcast(I32), 65535.0, gate_s[:, s],
                                               ALU.min, ALU.mult).then_inc(b_d, 1)

            def group_b(g):
                for n in range(UPG):
                    v = 12 * (g - 4) + 2 * n
                    dve.wait_ge(sig_d, NU + v + 1)
                    need(dve, b_d, v - 1)
                    round_sig(sigq, gate_in(2 * n % 6, True))
                    if not (isinstance(g, int) and g == 4 and n == 0):
                        up_max(g * UPG + n - 1, (n - 1) % 2)
                    act_int(6 * (g - 4) + n)
                    act_int_odd(6 * (g - 4) + n, (2 * n + 1) % 6, n % 2)

            for n in range(NU // 2):
                round_a(2 * n)
                up_max(n, n % 2)
                if n < UPG:
                    act_max(2 * n)
                    round_a(2 * n + 1)
                else:
                    round_a(2 * n + 1)
                    act_max(2 * n)
                act_max(2 * n + 1)
            dve.wait_ge(a_mx, NU)
            nc.vector.tensor_reduce(col["smx"], scol, AX.X, ALU.max).then_inc(col_max, 1)
            scalar2(col["su"], col["gsc"], 1.0 / 65536.0, 1.0)
            dve.wait_ge(col_all, 7)
            quant_scale("ssc", "sinv", "st", "src", "sall", col["su"]).then_inc(sinv_d, 1)
            dve.wait_ge(sinv_d, 1)
            group_b(4)
            with nc.vector.Fori(5, NG) as g:
                group_b(g)
            up_max(NU - 1, 1)
            dve.wait_ge(u_mx, NU)
            nc.vector.tensor_reduce(col["umx"], ucol, AX.X, ALU.max).then_inc(col_max, 1)
            dve.wait_ge(col_all, 8)
            quant_scale("usc", "uinv", "ut", "urc", "uall", col["fu"]).then_inc(uinv_d, 1)
            scalar2(col["oo"], col["ssc"], col["usc"], 1.0)

            def o_max(t, k):
                n = 12 * t + k
                if k % 4 == 0:
                    m = n // 4
                    dve.wait_ge(pu_d, m + 1)
                    nc.vector.tensor_tensor(ring5[:, k % 6], qa5[:, 0], Q[:, n], ALU.mult).then_inc(po_d, 1)
                    dve.wait_ge(po_d, m + 1)
                    nc.vector.tensor_reduce(ocol[:, 9 + m:10 + m], ring5[:, k % 6], AX.X, ALU.max,
                                            apply_absolute_value=True).then_inc(o_mx, 1)
                    return
                m = 3 * (n // 4) + k % 4 - 1
                dve.wait_ge(au_d, m + 1)
                dve.wait_ge(ag_d, m + 1)
                c = m % 9
                nc.vector.tensor_tensor_reduce(ring5[:, k % 6], qa5[:, k % 4], qb5[:, k % 4], 1.0, ocol[:, c:c + 1], ALU.mult,
                                               ALU.max, ocol[:, c:c + 1]).then_inc(o_mx, 1)

            for t in range(4):
                for k in range(12):
                    o_max(t, k)
            dve.wait_ge(o_mx, NU)
            nc.vector.tensor_reduce(col["omx"], ocol, AX.X, ALU.max).then_inc(col_max, 1)
            dve.wait_ge(col_all, 9)
            linked(quant_scale("osc", "oinv", "ot", "orc", "oall", col["oo"]))
            scalar2(col["fin"], col["osc"], col["pw2"], 1.0)

            def o_int(t, k):
                n = 12 * t + k
                s, c = k // UPG, 2 * (k % UPG)
                hi = OT[:, s, 0, c:c + 2].rearrange("p c t -> p (c t)")
                lo = OT[:, s, 1, c:c + 2].rearrange("p c t -> p (c t)")
                if k % UPG == 0:
                    need(dve, dn_mm, 2 * (2 * t + s) - 2)
                dve.wait_ge(uq_d, n + 1)
                nc.vector.scalar_tensor_tensor(qb[:, k % 2], qa[:, k % 2], col["oinv"], Q[:, n], ALU.mult,
                                               ALU.mult).then_inc(oq_d, 1)
                dve.wait_ge(oq_d, n + 1)
                nc.vector.tensor_copy(hi, qb[:, k % 2]).then_inc(ohi_d, 1)
                dve.wait_ge(ohi_d, n + 1)
                nc.vector.tensor_tensor(lo, qb[:, k % 2], hi, ALU.subtract).then_inc(olo_d, 1)

            def finish(g, s):
                for r in range(2):
                    dve.wait_ge(dn_mm, 2 * g + r + 1)
                    dve.wait_ge(x2_ld[r], 16 * g + 16)
                    nc.vector.scalar_tensor_tensor(x2_in[:, r], ps[:, 4 * s + 2 * r:4 * s + 2 * r + 2].rearrange("p b w -> p (b w)"),
                                                   col["fin"], x2_in[:, r], ALU.mult, ALU.add).then_inc(fin_d, 1)

            for k in range(UPG):
                o_int(0, k)
            for k in range(UPG, 2 * UPG):
                o_int(0, k)
            finish(0, 0)
            with nc.vector.Fori(1, 4) as t:
                for k in range(UPG):
                    o_int(t, k)
                finish(2 * t - 1, 1)
                for k in range(UPG, 2 * UPG):
                    o_int(t, k)
                finish(2 * t, 0)
            finish(NG - 1, 1)


_INS = ['x', 'ctx_1024', 'L0_xattn_Wq', 'L0_xattn_Wkv', 'L0_ffn_w_gate', 'L0_ffn_w_up', 'L0_ffn_w_down']
_OUTS = [((B, S, D), 'float32')]


def kernel(**inputs):
    import numpy as _np
    import concourse.bacc as _bacc
    from concourse import mybir as _mybir
    from concourse.bass_utils import run_bass_kernel_spmd as _run

    nc = _bacc.Bacc("TRN2", target_bir_lowering=False, num_devices=1)
    arrays, args = {}, []
    for name in _INS:
        a = _np.ascontiguousarray(inputs[name])
        arrays[f"in_{name}_dram"] = a
        args.append(nc.dram_tensor(f"in_{name}_dram", a.shape, _mybir.dt.from_np(a.dtype), kind="ExternalInput").ap())
    for i, (shape, dtype) in enumerate(_OUTS):
        dt = _mybir.dt.from_np(_np.dtype(dtype))
        args.append(nc.dram_tensor(f"out_{i}_dram", shape, dt, kind="ExternalOutput").ap())
    build(nc, *args)
    r = _run(nc, [arrays], core_ids=[0])
    got = tuple(r.results[0][f"out_{i}_dram"] for i in range(len(_OUTS)))
    return got[0]
```
